# Optimizing a Trainium2 kernel written in Bass

```python
import numpy as np
import jax
import jax.numpy as jnp

def _softmax(x, axis=-1):
    return jax.nn.softmax(x, axis=axis)

def _gelu(x):
    return jax.nn.gelu(x, approximate=True)

def _silu(x):
    return jax.nn.silu(x)

def _sigmoid(x):
    return jax.nn.sigmoid(x)

def _layernorm(x, axis=-1, eps=1e-05):
    m = jnp.mean(x, axis=axis, keepdims=True)
    v = jnp.var(x, axis=axis, keepdims=True)
    return (x - m) / jnp.sqrt(v + eps)

def _scatter_add(tgt, idx, src, axis=0):
    return tgt.at[idx].add(src)

def _segment_sum(src, seg, n):
    return jax.ops.segment_sum(src, seg, n)
kernel_name = 'mk_prb_d1_jaxref_r4_4f3c0f'

def setup_inputs(seed: int=0):
    np.random.seed(seed)
    _w = jnp.asarray

    def _L0_attn_setup():
        import jax, jax.numpy as jnp
        import numpy as np
        N_HEADS = 16
        MAX_DIST = 64
        key = jax.random.key(seed)
        ks = jax.random.split(key, 7)
        B, S, D = (16, 128, 256)
        hd = D // N_HEADS
        num_rel = 2 * MAX_DIST + 1
        s = 0.02
        return {'x': jax.random.normal(ks[0], (B, S, D), dtype=jnp.float32), 'Wq': jax.random.normal(ks[1], (D, D), dtype=jnp.float32) * s, 'Wk': jax.random.normal(ks[2], (D, D), dtype=jnp.float32) * s, 'Wv': jax.random.normal(ks[3], (D, D), dtype=jnp.float32) * s, 'Eq': jax.random.normal(ks[4], (num_rel, hd), dtype=jnp.float32) * s, 'Ek': jax.random.normal(ks[5], (num_rel, hd), dtype=jnp.float32) * s, 'Ev': jax.random.normal(ks[6], (num_rel, hd), dtype=jnp.float32) * s}
    _L0_attn_in = _L0_attn_setup()

    def _L0_ffn_setup():
        import jax, jax.numpy as jnp
        import numpy as np
        NUM_EXPERTS = 8
        NUM_SELECTED = 2
        EXPERT_CAPACITY = 128
        NUM_GROUPS = 8

        def _routing(xg, w_router):
            G, T, H = xg.shape
            logits = jnp.einsum('gth,he->gte', xg, w_router)
            probs = jax.nn.softmax(logits, axis=-1)
            _gate, idx = jax.lax.top_k(probs, NUM_SELECTED)
            idx_kt = jnp.swapaxes(idx, 1, 2).reshape(G, -1)
            expert_mask = jax.nn.one_hot(idx_kt, NUM_EXPERTS, dtype=jnp.int32)
            priority = jnp.cumsum(expert_mask, axis=1) * expert_mask - 1
            priority = priority.reshape(G, NUM_SELECTED, T, NUM_EXPERTS)
            priority = jnp.swapaxes(priority, 1, 2).max(axis=2)
            dispatch = jax.nn.one_hot(priority, EXPERT_CAPACITY, dtype=xg.dtype)
            combine = probs[..., None] * dispatch
            return (dispatch, combine)
        key = jax.random.key(seed)
        k1, k2, k3, k4 = jax.random.split(key, 4)
        B, S, H, F = (8, 512, 256, 1024)
        return {'x': jax.random.normal(k1, (B, S, H), jnp.float32), 'w_router': jax.random.normal(k2, (H, NUM_EXPERTS), jnp.float32) * 0.02, 'wi': jax.random.normal(k3, (NUM_EXPERTS, H, F), jnp.float32) * 0.02, 'wo': jax.random.normal(k4, (NUM_EXPERTS, F, H), jnp.float32) * 0.02}
    _L0_ffn_in = _L0_ffn_setup()
    _d = {'L0_attn_x': _L0_attn_in['x'], 'L0_attn_Wq': _L0_attn_in['Wq'], 'L0_attn_Wk': _L0_attn_in['Wk'], 'L0_attn_Wv': _L0_attn_in['Wv'], 'L0_attn_Eq': _L0_attn_in['Eq'], 'L0_attn_Ek': _L0_attn_in['Ek'], 'L0_attn_Ev': _L0_attn_in['Ev'], 'L0_ffn_w_router': _L0_ffn_in['w_router'], 'L0_ffn_wi': _L0_ffn_in['wi'], 'L0_ffn_wo': _L0_ffn_in['wo']}
    _x0 = _d['L0_attn_x']
    _d['L0_attn_x'] = jax.random.normal(jax.random.fold_in(jax.random.key(seed), 1), (8, 1024, 256), dtype=_x0.dtype)
    del _x0
    return _d

def reference(L0_attn_x, L0_attn_Wq, L0_attn_Wk, L0_attn_Wv, L0_attn_Eq, L0_attn_Ek, L0_attn_Ev, L0_ffn_w_router, L0_ffn_wi, L0_ffn_wo):

    def _L0_attn_ref(x, Wq, Wk, Wv, Eq, Ek, Ev):
        import jax, jax.numpy as jnp
        import numpy as np
        N_HEADS = 16
        MAX_DIST = 64
        B, S, D = x.shape
        H = N_HEADS
        hd = D // H
        r = jnp.arange(S)
        rel = jnp.clip(r[:, None] - r[None, :], -MAX_DIST, MAX_DIST) + MAX_DIST

        def proj(W):
            return jnp.einsum('bsd,de->bse', x, W).reshape(B, S, H, hd).transpose(0, 2, 1, 3)
        q, k, v = (proj(Wq), proj(Wk), proj(Wv))
        a_q = Eq[rel]
        a_k = Ek[rel]
        a_v = Ev[rel]
        content = jnp.einsum('bhld,bhmd->bhlm', q, k)
        rel_k = jnp.einsum('bhld,lmd->bhlm', q, a_k)
        rel_q = jnp.einsum('bhmd,lmd->bhlm', k, a_q)
        pos_pos = jnp.einsum('lmd,lmd->lm', a_q, a_k)
        scale = 1.0 / hd ** 0.5
        logits = (content + rel_k + rel_q + pos_pos) * scale
        attn = jax.nn.softmax(logits, axis=-1)
        out = jnp.einsum('bhlm,bhmd->bhld', attn, v) + jnp.einsum('bhlm,lmd->bhld', attn, a_v)
        return out.transpose(0, 2, 1, 3).reshape(B, S, D)

    def _L0_ffn_ref(x, w_router, wi, wo):
        import jax, jax.numpy as jnp
        import numpy as np
        NUM_EXPERTS = 8
        NUM_SELECTED = 2
        EXPERT_CAPACITY = 128
        NUM_GROUPS = 8

        def _routing(xg, w_router):
            G, T, H = xg.shape
            logits = jnp.einsum('gth,he->gte', xg, w_router)
            probs = jax.nn.softmax(logits, axis=-1)
            _gate, idx = jax.lax.top_k(probs, NUM_SELECTED)
            idx_kt = jnp.swapaxes(idx, 1, 2).reshape(G, -1)
            expert_mask = jax.nn.one_hot(idx_kt, NUM_EXPERTS, dtype=jnp.int32)
            priority = jnp.cumsum(expert_mask, axis=1) * expert_mask - 1
            priority = priority.reshape(G, NUM_SELECTED, T, NUM_EXPERTS)
            priority = jnp.swapaxes(priority, 1, 2).max(axis=2)
            dispatch = jax.nn.one_hot(priority, EXPERT_CAPACITY, dtype=xg.dtype)
            combine = probs[..., None] * dispatch
            return (dispatch, combine)
        B, S, H = x.shape
        T = B * S // NUM_GROUPS
        xg = x.reshape(NUM_GROUPS, T, H)
        dispatch, combine = _routing(xg, w_router)
        expert_in = jnp.einsum('gth,gtec->gech', xg, dispatch)
        h = jax.nn.gelu(jnp.einsum('gech,ehf->gecf', expert_in, wi))
        expert_out = jnp.einsum('gecf,efh->gech', h, wo)
        out = jnp.einsum('gech,gtec->gth', expert_out, combine)
        return out.reshape(B, S, H)
    x = L0_attn_x
    xn = _layernorm(x, axis=-1)
    x = x + _L0_attn_ref(xn, L0_attn_Wq, L0_attn_Wk, L0_attn_Wv, L0_attn_Eq, L0_attn_Ek, L0_attn_Ev) + _L0_ffn_ref(xn, L0_ffn_w_router, L0_ffn_wi, L0_ffn_wo)
    return x

_drawn_inputs = setup_inputs


def setup_inputs(seed=0):
    import zlib

    import numpy as np

    out = dict(_drawn_inputs(seed))
    spreads = {}
    factors = {'L0_attn_Wq': 8.0,
     'L0_attn_Wk': 8.0,
     'L0_attn_Wv': 5.299,
     'L0_attn_Eq': 8.0,
     'L0_attn_Ek': 8.0,
     'L0_attn_Ev': 3.396,
     'L0_ffn_w_router': 2.834,
     'L0_ffn_wi': 2.693}
    for name, (base, spread) in spreads.items():
        noise = np.random.default_rng([zlib.crc32(name.encode()), seed]).standard_normal(out[name].shape)
        drawn = base * np.exp(spread * noise) if base else spread * noise
        out[name] = jnp.asarray(drawn.astype(out[name].dtype))
    for name, factor in factors.items():
        out[name] = (out[name] * factor).astype(out[name].dtype)
    return out
```

```python
from contextlib import ExitStack

import concourse.bass as bass
import concourse.mybir as mybir
import numpy as np

F32, BF16 = mybir.dt.float32, mybir.dt.bfloat16
ALU, ACT, AX = mybir.AluOpType, mybir.ActivationFunctionType, mybir.AxisListType

P = 128
B, S, D = 8, 1024, 256
H, HD = 16, 16
NT = S // P
DH = D // P
E, CAP, F = 8, 128, 1024
FT = F // P
MAXD = 64
NH = B * H
GH = 4
NG = NH // GH
SLOTS = 6
KR = SLOTS * HD
QR = KR + 3
VW = HD + 1
WIN = 2 * P
PAD = 64
SCALE = 1.0 / HD ** 0.5
EPS = 1e-5
Q_SLOTS = (0, 0, 0, 1, 1, 2)
K_SLOTS = (2, 0, 1, 0, 1, 0)
Q128, Q0, K128, K0 = range(4)


def ge(eng, s, value):
    if not (isinstance(value, int) and value <= 0):
        eng.wait_ge(s, value)


def turns(eng, n, body):
    body(0)
    with eng.Fori(1, n) as k:
        body(k)


def dram(nc, name, shape, dt, kind="Internal"):
    return nc.dram_tensor(name, shape, dt, kind=kind).ap()


class Scratch:

    def __init__(self, nc):
        self.opnd = dram(nc, "opnd", (4, SLOTS, B, D, S), BF16)
        self.vals = dram(nc, "vals", (NH, P, NT, 2, VW), F32)
        self.pos = dram(nc, "pos", (B, P, NT * E), F32)
        self.prob = dram(nc, "prob", (B, P, NT * E), F32)
        self.ein = dram(nc, "ein", (E, DH, P, B, CAP), F32)
        self.eout = dram(nc, "eout", (B, CAP, E, D), F32)
        self.attn = dram(nc, "attn", (NH, P, NT * HD), F32)
        self.tabq = dram(nc, "tabq", (QR, P + 1), BF16)
        self.tabk = dram(nc, "tabk", (2, KR, 3 * P), BF16)
        self.tabv = dram(nc, "tabv", (2, P, VW), F32)
        self.skew = dram(nc, "skew", (4, P, NT, 2 * P), F32)
        self.prow = dram(nc, "prow", (8, P, WIN), F32)


def tables_phase(nc, sem, i, scr):
    with ExitStack() as ctx:
        sb = lambda n, s, d=F32: ctx.enter_context(nc.sbuf_tensor(n, s, d))
        NX, NU = P + 1, 3 * P
        ekx, eqx = sb("t_ekx", [KR, NX]), sb("t_eqx", [KR, NX])
        equ = sb("t_equ", [KR, NU])
        cols = sb("t_cols", [KR, 4])
        evx, ev128, ev0 = sb("t_evx", [P, HD]), sb("t_ev128", [P, HD]), sb("t_ev0", [P, HD])
        marks = sb("t_marks", [KR, 6])
        tq = sb("t_tq", [KR, NX])
        prod = sb("t_prod", [KR, NX])
        diff = sb("t_diff", [KR, 2])
        negd = sb("t_negd", [KR, 1])
        ones = sb("t_ones", [KR, 1])
        tk = sb("t_tk", [KR, 2, NU])
        hi, mid, lo = (sb(f"t_{n}", [KR, 2 * NU], BF16) for n in ("hi", "mid", "lo"))
        rest, mix = sb("t_rest", [KR, 2 * NU]), sb("t_mix", [KR, 2 * NU])
        outq, outk = sb("t_outq", [KR, NX], BF16), sb("t_outk", [KR, 2 * NU], BF16)
        crow, crest = sb("t_crow", [1, NX]), sb("t_crest", [1, NX])
        cpart = sb("t_cpart", [1, 3, NX], BF16)
        tv = sb("t_tv", [P, 2, VW])
        zero = sb("t_zero", [P, NT * 2 * P])
        pc = ctx.enter_context(nc.psum_tensor("t_pc", [P, 512], F32))
        loaded, zeroed, prod_ready, const_ready = sem("t_loaded"), sem("t_zeroed"), sem("t_prod"), sem("t_const")
        tables_ready, stored = sem("t_ready"), sem("t_stored")
        with nc.Block() as block:
            @block.sync
            def _(sp):
                for dst, src in ((ekx, i["ekx"]), (eqx, i["eqx"]), (equ, i["equ"]), (cols, i["eqk_cols"][0:KR]),
                                 (evx, i["evx"]), (ev128, i["ev_rows"][:, 0, 0:HD]), (ev0, i["ev_rows"][:, 1, 0:HD]),
                                 (marks, i["marks"])):
                    sp.dma_start(dst[:], src).then_inc(loaded, 16)
                sp.wait_ge(zeroed, 1)
                for n in range(4):
                    sp.dma_start(scr.skew[n].rearrange("p t n -> p (t n)"), zero[:]).then_inc(stored, 16)
                sp.wait_ge(tables_ready, 1)
                sp.dma_start(scr.tabq[0:KR, :], outq[:]).then_inc(stored, 16)
                sp.dma_start(scr.tabq[KR:QR, :].rearrange("(a r) n -> a r n", a=1), cpart[:]).then_inc(stored, 16)
                sp.dma_start(scr.tabk.rearrange("c k n -> k c n"), outk[:].rearrange("k (c n) -> k c n", c=2)).then_inc(stored, 16)
                sp.dma_start(scr.tabv.rearrange("c p n -> p c n"), tv[:]).then_inc(stored, 16)
                sp.wait_ge(stored, 16 * 8)

            @block.tensor
            def _(pe):
                pe.wait_ge(prod_ready, 1)
                nc.tensor.matmul(pc[0:1, 0:NX], ones[0:HD, :], prod[0:HD, :], start=True, stop=True).then_inc(const_ready, 1)

            @block.vector
            def _(dve):
                v = nc.vector
                v.memset(zero[:], 0.0).then_inc(zeroed, 1)
                v.memset(ones[:], 1.0)
                v.memset(tv[:], 0.0)
                dve.wait_ge(loaded, 16 * 8)
                dve.drain()
                v.tensor_tensor(diff[:, 0:1], cols[:, 0:1], cols[:, 1:2], ALU.subtract)
                v.tensor_tensor(diff[:, 1:2], cols[:, 2:3], cols[:, 3:4], ALU.subtract)
                v.tensor_scalar(tq[:, 0:P], ekx[:, 0:P], cols[:, 2:3], None, ALU.subtract)
                v.tensor_scalar(prod[:, 0:P], eqx[:, 0:P], cols[:, 0:1], SCALE, ALU.subtract, ALU.mult)
                v.tensor_scalar(tk[:, 0, :], equ[:], cols[:, 0:1], SCALE, ALU.subtract, ALU.mult)
                v.tensor_scalar(tk[:, 1, :], equ[:], cols[:, 1:2], SCALE, ALU.subtract, ALU.mult)
                v.tensor_scalar(tv[:, 0, 0:HD], evx[:], 1.0, None, ALU.mult)
                dve.drain()
                v.tensor_copy(tq[:, P:NX], diff[:, 1:2])
                v.tensor_scalar(negd[:], diff[:, 0:1], -SCALE, None, ALU.mult)
                v.tensor_tensor(tv[:, 0, 0:HD], evx[:], ev0[:], ALU.subtract)
                v.tensor_tensor(tv[:, 1, 0:HD], ev128[:], ev0[:], ALU.subtract)
                dve.drain()
                v.tensor_tensor(prod[:, 0:P], prod[:, 0:P], tq[:, 0:P], ALU.mult)
                v.tensor_tensor(prod[:, P:NX], negd[:], diff[:, 1:2], ALU.mult).then_inc(prod_ready, 1)

                def split(src, n, marks3, out):
                    dve.drain()
                    v.tensor_copy(hi[:, 0:n], src)
                    dve.drain()
                    v.tensor_tensor(rest[:, 0:n], src, hi[:, 0:n], ALU.subtract)
                    dve.drain()
                    v.tensor_copy(mid[:, 0:n], rest[:, 0:n])
                    dve.drain()
                    v.tensor_tensor(lo[:, 0:n], rest[:, 0:n], mid[:, 0:n], ALU.subtract)
                    v.tensor_scalar(mix[:, 0:n], hi[:, 0:n], marks3[:, 0:1], None, ALU.mult)
                    dve.drain()
                    v.scalar_tensor_tensor(rest[:, 0:n], mid[:, 0:n], marks3[:, 1:2], mix[:, 0:n], ALU.mult, ALU.add)
                    dve.drain()
                    v.scalar_tensor_tensor(out, lo[:, 0:n], marks3[:, 2:3], rest[:, 0:n], ALU.mult, ALU.add)

                split(tq[:], NX, marks[:, 3:6], outq[:])
                split(tk[:].rearrange("k c n -> k (c n)"), 2 * NU, marks[:, 0:3], outk[:])
                dve.wait_ge(const_ready, 1)
                v.tensor_copy(crow[:], pc[0:1, 0:NX])
                dve.drain()
                v.tensor_copy(cpart[:, 0, :], crow[:])
                dve.drain()
                v.tensor_tensor(crest[:], crow[:], cpart[:, 0, :], ALU.subtract)
                dve.drain()
                v.tensor_copy(cpart[:, 1, :], crest[:])
                dve.drain()
                v.tensor_tensor(cpart[:, 2, :], crest[:], cpart[:, 1, :], ALU.subtract)
                dve.drain()
                dve.sem_inc(tables_ready, 1)


def tokens_phase(nc, sem, i, scr):
    with ExitStack() as ctx:
        sb = lambda n, s, d=F32: ctx.enter_context(nc.sbuf_tensor(n, s, d))
        xt, xn = sb("a_x", [P, NT, D]), sb("a_xn", [P, NT, D])
        xnT = sb("a_xnT", [P, DH, S])
        wq, wk, wv = (sb(f"a_{n}", [P, DH, D]) for n in ("wq", "wk", "wv"))
        wr = sb("a_wr", [P, DH, E])
        ident = sb("a_ident", [P, P])
        cols = sb("a_cols", [P, 4])
        evrow = sb("a_evrow", [P, 2, D])
        iota_c, iota_e = sb("a_iota_c", [P, CAP]), sb("a_iota_e", [P, NT * E])
        upper = sb("a_upper", [P, 2 * P])
        tri = sb("a_tri", [P, 2 * P], BF16)
        stats, mv = sb("a_stats", [P, NT, 6]), sb("a_mv", [P, NT, 2])
        std, rstd = sb("a_std", [P, NT]), sb("a_rstd", [P, NT])
        proj = sb("a_proj", [P, 2, S])
        hi, mid, lo = (sb(f"a_{n}", [P, 2, S], BF16) for n in ("hi", "mid", "lo"))
        rest = sb("a_rest", [P, 2, S])
        vb = sb("a_vb", [P, H, NT, 2, VW])
        lmax, lsub, lexp, prob = (sb(f"a_{n}", [P, NT, E]) for n in ("lmax", "lsub", "lexp", "prob"))
        red, rsum = sb("a_red", [P, NT]), sb("a_rsum", [P, NT])
        same, cand, left = (sb(f"a_{n}", [P, NT, E]) for n in ("same", "cand", "left"))
        pick = sb("a_pick", [P, 2, NT, E])
        pickb = sb("a_pickb", [P, 2 * NT, E], BF16)
        prk = sb("a_prk", [P, 2, NT * E])
        pos = sb("a_pos", [P, NT * E])
        disp = sb("a_disp", [P, 2, E * CAP])
        ein = sb("a_ein", [P, DH, E * CAP])
        ps = [ctx.enter_context(nc.psum_tensor(f"a_ps{n}", [P, 512], F32)) for n in range(8)]
        big = ps[0:4]
        pproj, prt = ps[4:6], ps[7]

        w_in, x_in = sem("a_w_in"), sem("a_x_in")
        carrier = sem("a_carrier")
        tri_ready, var_ready, std_ready, xn_ready = (sem(f"a_{n}") for n in ("tri", "var", "stdr", "xnr"))
        t_done, t_evac = sem("a_t_done"), sem("a_t_evac")
        lg_done, lsub_ready, exp_ready = (sem(f"a_{n}") for n in ("lg", "lsubr", "expr"))
        pick_ready, rank_done, pos_ready, pos_out = (sem(f"a_{n}") for n in ("pickr", "rank", "posr", "poso"))
        disp_ready, disp_used, in_done, in_evac, ein_out = (sem(f"a_{n}") for n in ("dispr", "dispu", "ind", "ine", "eino"))
        v_done, v_evac, vals_out = sem("a_v_done"), sem("a_v_evac"), sem("a_vals_out")
        pr_done, proj_ready, hi_ready, rest_ready, mid_ready, lo_ready, parts_out = (
            sem(f"a_{n}") for n in ("prd", "projr", "hir", "restr", "midr", "lor", "partso"))
        NL = 14
        units = [(w, op, h) for w, op in ((wq, Q128), (wk, K128)) for h in range(DH)]
        NUN = len(units)

        with nc.Block() as block:
            @block.sync
            def _(sp):
                loads = [(wq[:, h, :], i["wq"][h * P:(h + 1) * P, :]) for h in range(DH)]
                loads += [(wk[:, h, :], i["wk"][h * P:(h + 1) * P, :]) for h in range(DH)]
                loads += [(wv[:, h, :], i["wv"][h * P:(h + 1) * P, :]) for h in range(DH)]
                loads += [(wr[:, h, :], i["wr"][h * P:(h + 1) * P, :]) for h in range(DH)]
                loads += [(ident[:], i["ident"]), (cols[:], i["eqk_cols"]), (evrow[:], i["ev_rows"]),
                          (iota_c[:], i["iota_c"]), (iota_e[:], i["iota_e"]), (upper[:], i["upper"])]
                assert len(loads) == NL
                for dst, src in loads:
                    sp.dma_start(dst, src).then_inc(w_in, 16)
                def body(b):
                    ge(sp, xn_ready, b)
                    for k in range(2):
                        sp.dma_start(xt[:, 4 * k:4 * k + 4, :], i["x"][b, k * S // 2:(k + 1) * S // 2].rearrange(
                            "(t p) d -> p t d", p=P)).then_inc(x_in, 16)
                    ge(sp, pos_ready, b + 1)
                    sp.dma_start(scr.pos[b], pos[:]).then_inc(pos_out, 16)
                    sp.dma_start(scr.prob[b], prob[:].rearrange("p t e -> p (t e)")).then_inc(pos_out, 16)
                    ge(sp, v_evac, NT * (b + 1))
                    sp.dma_start(scr.vals.rearrange("(b h) p t c n -> b p h (t c n)", b=B)[b],
                                 vb[:].rearrange("p h t c n -> p h (t c n)")).then_inc(vals_out, 16)
                    for u, (_, op, h) in enumerate(units):
                        ge(sp, lo_ready, NUN * b + u + 1)
                        sp.sem_inc(carrier, 1)
                        for c in range(2):
                            dst = scr.opnd[op + c].rearrange("s b e n -> b e s n")[b, h * P:(h + 1) * P]
                            slots = Q_SLOTS if op == Q128 else K_SLOTS
                            for part, src in enumerate((hi, mid, lo)):
                                at = [s for s in range(SLOTS) if slots[s] == part]
                                step = at[1] - at[0] if len(at) > 1 else 1
                                sp.dma_start(dst[:, at[0]:at[-1] + 1:step, :],
                                             src[:, c:c + 1, :].to_broadcast([P, len(at), S])).then_inc(parts_out, 16)
                    ge(sp, in_evac, 4 * (b + 1))
                    for h in range(DH):
                        sp.dma_start(scr.ein[:, h].rearrange("e p b c -> b p e c")[b],
                                     ein[:, h, :].rearrange("p (e c) -> p e c", e=E)).then_inc(ein_out, 16)

                turns(sp, B, body)
                sp.wait_ge(pos_out, 32 * B)
                sp.wait_ge(vals_out, 16 * B)
                sp.wait_ge(parts_out, 96 * NUN * B)
                sp.wait_ge(ein_out, 32 * B)

            @block.tensor
            def _(pe):
                t = nc.tensor
                pe.wait_ge(w_in, 16 * NL)
                pe.wait_ge(tri_ready, 1)
                def body(b):
                    ge(pe, xn_ready, b + 1)
                    ge(pe, in_evac, 4 * b)
                    for h in range(DH):
                        for half in range(2):
                            for n in range(4):
                                last = t.transpose(big[2 * h + half][:, n * P:(n + 1) * P],
                                                   xn[:, 4 * half + n, h * P:(h + 1) * P], ident[:])
                            last.then_inc(t_done, 1)
                    ge(pe, t_evac, 4 * (b + 1))
                    ge(pe, pos_ready, b)
                    for n in range(NT):
                        for h in range(DH):
                            last = t.matmul(prt[:, n * E:(n + 1) * E], xnT[:, h, n * P:(n + 1) * P], wr[:, h, :],
                                            start=h == 0, stop=h == DH - 1)
                    last.then_inc(lg_done, 1)
                    for n in range(NT):
                        if n >= 2:
                            ge(pe, v_evac, NT * b + n - 1)
                        elif n == 0:
                            ge(pe, proj_ready, NUN * b)
                        for h in range(DH):
                            last = t.matmul(pproj[n % 2][:, 0:D], xnT[:, h, n * P:(n + 1) * P], wv[:, h, :],
                                            start=h == 0, stop=h == DH - 1)
                        last.then_inc(v_done, 1)
                    for u, (w, _, eh) in enumerate(units):
                        if u == 0:
                            ge(pe, v_evac, NT * (b + 1))
                        else:
                            ge(pe, proj_ready, NUN * b + u)
                        for half in range(2):
                            for h in range(DH):
                                last = t.matmul(pproj[half][:], w[:, h, eh * P:(eh + 1) * P],
                                                xnT[:, h, half * 512:(half + 1) * 512], start=h == 0, stop=h == DH - 1)
                        last.then_inc(pr_done, 1)
                        if u == 0:
                            ge(pe, pick_ready, b + 1)
                            t.matmul(prt[:, 0:2 * NT * E], tri[:, 0:P], pickb[:].rearrange("p k e -> p (k e)"),
                                     start=True, stop=False)
                            for k in range(2 * NT - 1):
                                n = 2 * NT - 1 - k
                                last = t.matmul(prt[:, (k + 1) * E:2 * NT * E], tri[:, P:2 * P],
                                                pickb[:, k:k + 1, :].to_broadcast([P, n, E]),
                                                start=False, stop=k == 2 * NT - 2)
                            last.then_inc(rank_done, 1)
                    for n in range(NT):
                        ge(pe, disp_ready, NT * b + n + 1)
                        for h in range(DH):
                            for half in range(2):
                                last = t.matmul(big[2 * h + half][:], xn[:, n, h * P:(h + 1) * P],
                                                disp[:, n % 2, half * 512:(half + 1) * 512],
                                                start=n == 0, stop=n == NT - 1)
                        last.then_inc(disp_used, 1)

                turns(pe, B, body)

            @block.scalar
            def _(act):
                a = nc.scalar
                def body(b):
                    ge(act, var_ready, b + 1)
                    a.activation(std[:], std[:], ACT.Sqrt).then_inc(std_ready, 1)
                    for k in range(4):
                        ge(act, t_done, 4 * b + k + 1)
                        a.copy(xnT[:, k // 2, (k % 2) * 512:(k % 2 + 1) * 512], big[k][:]).then_inc(t_evac, 1)
                    ge(act, lsub_ready, b + 1)
                    a.activation(lexp[:], lsub[:], ACT.Exp).then_inc(exp_ready, 1)
                    for u in range(NUN):
                        ge(act, proj_ready, NUN * b + u + 1)
                        ge(act, parts_out, 96 * (NUN * b + u))
                        a.copy(hi[:], proj[:]).then_inc(hi_ready, 1)
                        ge(act, rest_ready, NUN * b + u + 1)
                        a.copy(mid[:], rest[:]).then_inc(mid_ready, 1)
                    ge(act, ein_out, 32 * b)
                    ge(act, disp_used, NT * (b + 1))
                    for k in range(4):
                        a.copy(ein[:, k // 2, (k % 2) * 512:(k % 2 + 1) * 512], big[k][:]).then_inc(in_evac, 1)

                turns(act, B, body)

            @block.gpsimd
            def _(pool):
                def body(b):
                    for u in range(NUN):
                        ge(pool, hi_ready, NUN * b + u + 1)
                        nc.gpsimd.tensor_tensor(rest[:], proj[:], hi[:], ALU.subtract).then_inc(rest_ready, 1)
                        ge(pool, mid_ready, NUN * b + u + 1)
                        nc.gpsimd.tensor_tensor(lo[:], rest[:], mid[:], ALU.subtract).then_inc(lo_ready, 1)

                turns(pool, B, body)

            @block.vector
            def _(dve):
                v = nc.vector
                dve.wait_ge(w_in, 16 * NL)
                v.tensor_copy(tri[:], upper[:]).then_inc(tri_ready, 1)
                v.memset(vb[:], 1.0)
                row = lambda ap: ap[:].rearrange("p (t a) -> p t a", a=1).to_broadcast([P, NT, E])
                ie = iota_e[:].rearrange("p (t e) -> p t e", e=E)
                def body(b):
                    ge(dve, x_in, 32 * (b + 1))
                    for n in range(NT):
                        v.bn_stats(stats[:, n, :], xt[:, n, :])
                    dve.drain()
                    for n in range(NT):
                        v.bn_aggr(mv[:, n, :], stats[:, n, :])
                    dve.drain()
                    v.tensor_scalar(std[:], mv[:, :, 1], EPS, None, ALU.add).then_inc(var_ready, 1)
                    ge(dve, std_ready, b + 1)
                    v.reciprocal(rstd[:], std[:])
                    dve.drain()
                    ge(dve, disp_used, NT * b)
                    for n in range(NT):
                        ins = v.tensor_scalar(xn[:, n, :], xt[:, n, :], mv[:, n, 0:1], rstd[:, n:n + 1],
                                              ALU.subtract, ALU.mult)
                    ins.then_inc(xn_ready, 1)
                    ge(dve, lg_done, b + 1)
                    lg = prt[:, 0:NT * E].rearrange("p (t e) -> p t e", e=E)
                    v.tensor_reduce(red[:], lg, AX.X, ALU.max)
                    dve.drain()
                    v.tensor_tensor(lsub[:], lg, row(red), ALU.subtract).then_inc(lsub_ready, 1)
                    ge(dve, exp_ready, b + 1)
                    v.tensor_reduce(rsum[:], lexp[:], AX.X, ALU.add)
                    dve.drain()
                    v.reciprocal(rsum[:], rsum[:])
                    dve.drain()
                    ge(dve, pos_out, 32 * b)
                    v.tensor_tensor(prob[:], lexp[:], row(rsum), ALU.mult)
                    dve.drain()
                    for k in range(2):
                        src = prob if k == 0 else left
                        v.tensor_reduce(red[:], src[:], AX.X, ALU.max)
                        dve.drain()
                        v.tensor_tensor(same[:], src[:], row(red), ALU.is_equal)
                        dve.drain()
                        v.scalar_tensor_tensor(cand[:], same[:], -float(E), ie, ALU.mult, ALU.add)
                        dve.drain()
                        v.tensor_reduce(red[:], cand[:], AX.X, ALU.min)
                        dve.drain()
                        v.tensor_scalar(red[:], red[:], float(E), None, ALU.add)
                        dve.drain()
                        v.tensor_tensor(pick[:, k], ie, row(red), ALU.is_equal)
                        dve.drain()
                        if k == 0:
                            v.scalar_tensor_tensor(left[:], pick[:, 0], -4.0, prob[:], ALU.mult, ALU.add)
                            dve.drain()
                    v.tensor_copy(pickb[:], pick[:].rearrange("p k t e -> p (k t) e")).then_inc(pick_ready, 1)
                    ge(dve, vals_out, 16 * b)
                    for n in range(NT):
                        ge(dve, v_done, NT * b + n + 1)
                        src = pproj[n % 2][:, 0:D].rearrange("p (h d) -> p h d", h=H)
                        for c in range(2):
                            ins = v.tensor_tensor(vb[:, :, n, c, 0:HD], src,
                                                  evrow[:, c, :].rearrange("p (h d) -> p h d", h=H), ALU.add)
                        ins.then_inc(v_evac, 1)
                    for u, (_, op, _) in enumerate(units):
                        ge(dve, pr_done, NUN * b + u + 1)
                        ge(dve, lo_ready, NUN * b + u)
                        for c in range(2):
                            for half in range(2):
                                dst = proj[:, c, half * 512:(half + 1) * 512]
                                if op == Q128:
                                    ins = v.tensor_scalar(dst, pproj[half][:], cols[:, c:c + 1], SCALE, ALU.add, ALU.mult)
                                else:
                                    ins = v.tensor_scalar(dst, pproj[half][:], cols[:, 2 + c:3 + c], None, ALU.add)
                        ins.then_inc(proj_ready, 1)
                        if u == 1:
                            ge(dve, rank_done, b + 1)
                            v.tensor_tensor(prk[:].rearrange("p k n -> p (k n)"), prt[:, 0:2 * NT * E],
                                            pick[:].rearrange("p k t e -> p (k t e)"), ALU.mult)
                            dve.drain()
                            v.scalar_tensor_tensor(pos[:], prk[:, 0, :], -1.0, prk[:, 1, :], ALU.add, ALU.add).then_inc(pos_ready, 1)
                    dve.drain()
                    for n in range(NT):
                        if n >= 2:
                            ge(dve, disp_used, NT * b + n - 1)
                        for e in range(E):
                            ins = v.tensor_scalar(disp[:, n % 2, e * CAP:(e + 1) * CAP], iota_c[:],
                                                  pos[:, n * E + e:n * E + e + 1], None, ALU.is_equal)
                        ins.then_inc(disp_ready, 1)

                turns(dve, B, body)


def experts_phase(nc, sem, i, scr):
    GC = B * CAP
    with ExitStack() as ctx:
        sb = lambda n, s, d=F32: ctx.enter_context(nc.sbuf_tensor(n, s, d))
        wi = [sb(f"e_wi{n}", [P, DH, F]) for n in range(2)]
        wo = [sb(f"e_wo{n}", [P, FT, D]) for n in range(2)]
        xin = [sb(f"e_xin{n}", [P, DH, GC]) for n in range(2)]
        hid = sb("e_hid", [P, FT, GC])
        res = sb("e_res", [P, B, D])
        ph = [ctx.enter_context(nc.psum_tensor(f"e_ph{n}", [P, 512], F32)) for n in range(4)]
        po = [ctx.enter_context(nc.psum_tensor(f"e_po{n}", [P, 512], F32)) for n in range(4)]
        e_in = [sem("e_in0"), sem("e_in1")]
        h_done, h_ready, o_done, o_ready, res_out = (sem(f"e_{n}") for n in ("hd", "hr", "od", "or", "ro"))
        UH, UO = 2 * FT, B

        with nc.Block() as block:
            @block.sync
            def _(sp):
                def load(e, s):
                    for h in range(DH):
                        sp.dma_start(wi[s][:, h, :], i["wi"][e, h * P:(h + 1) * P, :]).then_inc(e_in[s], 16)
                        sp.dma_start(xin[s][:, h, :], scr.ein[e, h].rearrange("p b c -> p (b c)")).then_inc(e_in[s], 16)
                    for k in range(2):
                        sp.dma_start(wo[s][:, 4 * k:4 * k + 4, :], i["wo"][e, k * F // 2:(k + 1) * F // 2].rearrange(
                            "(t p) d -> p t d", p=P)).then_inc(e_in[s], 16)

                load(0, 0)
                load(1, 1)
                def store(e):
                    ge(sp, o_ready, UO * (e + 1))
                    sp.dma_start(scr.eout.rearrange("b c e d -> e c b d")[e], res[:]).then_inc(res_out, 16)

                def body(pair):
                    for s in range(2):
                        store(2 * pair + s)
                        load(2 * pair + s + 2, s)

                turns(sp, E // 2 - 1, body)
                store(E - 2)
                store(E - 1)
                sp.wait_ge(res_out, 16 * E)

            @block.tensor
            def _(pe):
                t = nc.tensor
                def body(pair):
                    for s in range(2):
                        e = 2 * pair + s
                        ge(pe, e_in[s], 96 * (pair + 1))
                        for f in range(FT):
                            for half in range(2):
                                k = 2 * f + half
                                if k >= 4:
                                    ge(pe, h_ready, UH * e + k - 3)
                                for h in range(DH):
                                    last = t.matmul(ph[k % 4][:], wi[s][:, h, f * P:(f + 1) * P],
                                                    xin[s][:, h, half * 512:(half + 1) * 512],
                                                    start=h == 0, stop=h == DH - 1)
                                last.then_inc(h_done, 1)
                        ge(pe, h_ready, UH * (e + 1))
                        for g in range(B):
                            ge(pe, o_ready, UO * e + max(0, g - 3))
                            for f in range(FT):
                                last = t.matmul(po[g % 4][:, 0:D], hid[:, f, g * CAP:(g + 1) * CAP], wo[s][:, f, :],
                                                start=f == 0, stop=f == FT - 1)
                            last.then_inc(o_done, 1)

                turns(pe, E // 2, body)

            @block.scalar
            def _(act):
                def body(e):
                    ge(act, o_done, UO * e)
                    for k in range(UH):
                        ge(act, h_done, UH * e + k + 1)
                        nc.scalar.activation(hid[:, k // 2, (k % 2) * 512:(k % 2 + 1) * 512], ph[k % 4][:],
                                             ACT.Gelu_apprx_tanh).then_inc(h_ready, 1)

                turns(act, E, body)

            @block.vector
            def _(dve):
                def body(e):
                    ge(dve, res_out, 16 * e)
                    for g in range(B):
                        ge(dve, o_done, UO * e + g + 1)
                        nc.vector.tensor_copy(res[:, g, :], po[g % 4][:, 0:D]).then_inc(o_ready, 1)

                turns(dve, E, body)


LT, LU, LP = 2, 4, 5
NR = 4
ST = GH * NT
QL_PER_STEP = 3
QL_STEPS = -(-ST // QL_PER_STEP)
RQ_FROM = 14
RQ_W = 16
NCH = WIN // RQ_W


def attend_phase(nc, sem, i, scr):
    with ExitStack() as ctx:
        sb = lambda n, s, d=F32: ctx.enter_context(nc.sbuf_tensor(n, s, d))
        k128 = sb("d_k128", [KR, 2, GH, S + 2 * PAD], BF16)
        q128 = sb("d_q128", [QR, 2, GH, S], BF16)
        k0, q0 = sb("d_k0", [KR, 2, S], BF16), sb("d_q0", [KR, 2, S], BF16)
        vals = sb("d_vals", [P, 2, NT, 2, VW])
        band = sb("d_band", [P, 2, GH, NT, WIN])
        qlin = sb("d_qlin", [P, 2, NT, P])
        prob = sb("d_prob", [P, NR, S + 2 * PAD])
        probT = sb("d_probT", [P, NR, NT, P])
        farm, far = sb("d_farm", [P, 2, P]), sb("d_far", [P, NR, P])
        near, nearT = sb("d_near", [P, NR, P]), sb("d_nearT", [P, 2, P])
        nmax = sb("d_nmax", [P, NR])
        rz, out = sb("d_rz", [P, 2, NT]), sb("d_out", [P, 2, NT, HD])
        ident, qmask, fmask = sb("d_ident", [P, P]), sb("d_qmask", [P, P]), sb("d_fmask", [P, 2, P])
        tabq, tabk, tabv = sb("d_tabq", [QR, P + 1], BF16), sb("d_tabk", [KR, 2, 3 * P], BF16), sb("d_tabv", [P, 2, VW])
        lg = [ctx.enter_context(nc.psum_tensor(f"d_lg{n}", [P, S], F32)) for n in range(2)]
        tp = [ctx.enter_context(nc.psum_tensor(f"d_tp{n}", [P, 512], F32)) for n in range(2)]
        po = ctx.enter_context(nc.psum_tensor("d_po", [P, 512], F32))
        pk = ctx.enter_context(nc.psum_tensor("d_pk", [P, 512], F32))
        o = po[:, 0:NT * VW].rearrange("p (t v) -> p t v", t=NT)
        ql = pk[:, 0:QL_PER_STEP * (P + 1)].rearrange("p (k x) -> p k x", k=QL_PER_STEP)

        consts, cleared = sem("d_consts"), sem("d_cleared")
        carrier = sem("d_carrier")
        group_in = sem("d_group_in")
        head_in = [sem(f"d_head_in{n}") for n in range(2)]
        val_in = [sem(f"d_val_in{n}") for n in range(2)]
        ql_done, ql_ready = sem("d_ql_done"), sem("d_ql_ready")
        skew_out = [sem(f"d_skew_out{n}") for n in range(GH)]
        skew_in = sem("d_skew_in")
        rq_done, band_ready = sem("d_rq_done"), sem("d_band_ready")
        lg_done, lg_added, max_ready, prob_ready = (sem(f"d_{n}") for n in ("lgd", "lga", "maxr", "probr"))
        tp_done, tp_read, near_done, near_read = (sem(f"d_{n}") for n in ("tpd", "tpr", "neard", "nearr"))
        win_out = [sem(f"d_win_out{n}") for n in range(NR)]
        near_in = [sem(f"d_near_in{n}") for n in range(NR)]
        far_ready, pv_done, out_ready = (sem(f"d_{n}") for n in ("farr", "pvd", "outr"))
        out_stored = [sem(f"d_out_stored{n}") for n in range(2)]
        const_loads = [(ident[:], i["ident"]), (qmask[:], i["qmask"]), (fmask[:], i["fmask"]), (tabq[:], scr.tabq),
                       (tabk[:], scr.tabk.rearrange("c k n -> k c n")), (tabv[:], scr.tabv.rearrange("c p n -> p c n"))]

        def window(t):
            a, z = max(0, t * P - PAD), min(S, t * P + P + PAD)
            return a, z, a - (t * P - PAD)

        def opnd_rows(op, g, j):
            return bass.AP(scr.opnd.tensor, op * SLOTS * B * D * S + (GH * g + j) * (HD * S),
                           [[B * D * S, SLOTS], [S, HD], [1, S]])

        def over_groups(eng, main, prefetch):
            for n in range(ST):
                prefetch(0, n, 0)

            def steps(g, par):
                for n in range(ST):
                    main(g, n, par, ST)
                    prefetch(g + 1, n, 1 - par)

            steps(0, 0)
            with eng.Fori(0, (NG - 2) // 2) as pair:
                steps(2 * pair + 1, 1)
                steps(2 * pair + 2, 0)
            for n in range(ST + LP + 2):
                main(NG - 1, n, 1, ST + LP + 2)

        def lag(g, n, by):
            k = n - by
            return None if k >= ST or (isinstance(g, int) and g == 0 and k < 0) else k

        with nc.Block() as block:
            @block.sync
            def _(sp):
                def load_group(g, par):
                    for j in range(GH):
                        sp.dma_start(q128[0:KR, par, j, :], opnd_rows(Q128, g, j)).then_inc(group_in, 16)
                        sp.dma_start(k128[:, par, j, PAD:PAD + S], opnd_rows(K128, g, j)).then_inc(group_in, 16)

                def load_head(g, j):
                    sp.dma_start(q0[:, j % 2, :], opnd_rows(Q0, g, j)).then_inc(head_in[j % 2], 16)
                    sp.dma_start(k0[:, j % 2, :], opnd_rows(K0, g, j)).then_inc(head_in[j % 2], 16)

                def load_vals(g, j):
                    sp.dma_start(vals[:, j % 2].rearrange("p t c n -> p (t c n)"),
                                 scr.vals.rearrange("g p t c n -> g p (t c n)")[GH * g + j]).then_inc(val_in[j % 2], 16)

                def prefetch(g, n, par):
                    if n == 0:
                        ge(sp, lg_done, ST * (g - 1))
                        load_group(g, par)
                    for j in range(GH):
                        at = -(-NT * (j + 1) // QL_PER_STEP) + 1
                        if n == at:
                            sp.wait_ge(ql_ready, QL_STEPS * g + at - 1)
                            sp.dma_start(scr.skew[j][:, :, 0:P], qlin[:, j % 2]).then_inc(skew_out[j], 16)
                        if n == at + 1:
                            ge(sp, lg_added, ST * (g - 1))
                            sp.wait_ge(skew_out[j], 16 * (g + 1))
                            for k in range(4):
                                src = bass.AP(scr.skew.tensor, (j * P + 32 * k) * NT * 2 * P,
                                              [[NT * 2 * P - 1, 32], [2 * P, NT], [1, P + 32]])
                                sp.dma_start(band[32 * k:32 * k + 32, par, j, :, 32 * k:32 * k + P + 32],
                                             src).then_inc(skew_in, 16)

                def main(g, n, par, end):
                    j = n // NT
                    if n < ST and n % NT == 0 and not (end > ST and j == GH - 1):
                        ge(sp, lg_done, ST * g + n)
                        load_head(g + (j + 1) // GH, (j + 1) % GH)
                    if n < ST and n % NT == LP and not (end > ST and j == GH - 1):
                        ge(sp, pv_done, ST * g + NT * j)
                        load_vals(g + (j + 1) // GH, (j + 1) % GH)
                    if n < ST:
                        if not (isinstance(g, int) and g == 0 and n < NT):
                            sp.wait_ge(near_in[n % NR], 16 * (ST // NR * g + n // NR - 1))
                            sp.sem_inc(carrier, 1)
                        sp.wait_ge(prob_ready, ST * g + n + 1)
                        sp.dma_start(scr.prow[n % NT], prob[:, n % NR, (n % NT) * P:(n % NT) * P + WIN]
                                     ).then_inc(win_out[n % NR], 16)
                    k = lag(g, n, 1)
                    if k is not None:
                        ge(sp, near_done, ST * g + k - NR + 1)
                        sp.sem_inc(carrier, 1)
                        sp.wait_ge(win_out[k % NR], 16 * (ST // NR * g + k // NR + 1))
                        src = bass.AP(scr.prow.tensor, (k % NT) * P * WIN, [[WIN + 1, P], [1, P]])
                        sp.dma_start(near[:, k % NR, :], src).then_inc(near_in[k % NR], 16)
                    k = lag(g, n, LP + 1)
                    if k is not None and k % NT == NT - 1:
                        sp.wait_ge(out_ready, GH * g + k // NT + 1)
                        sp.sem_inc(carrier, 1)
                        sp.dma_start(scr.attn[GH * g + k // NT], out[:, (k // NT) % 2].rearrange("p t d -> p (t d)")
                                     ).then_inc(out_stored[(k // NT) % 2], 16)

                for dst, src in const_loads:
                    sp.dma_start(dst, src).then_inc(consts, 16)
                load_head(0, 0)
                load_vals(0, 0)
                sp.wait_ge(cleared, 1)
                over_groups(sp, main, prefetch)
                for k in range(2):
                    sp.wait_ge(out_stored[k], 16 * NH // 2)

            @block.tensor
            def _(pe):
                t = nc.tensor

                def prefetch(g, n, par):
                    tiles = range(QL_PER_STEP * n, min(ST, QL_PER_STEP * (n + 1)))
                    k = n - RQ_FROM
                    if tiles or 0 <= k < NCH:
                        ge(pe, ql_ready, QL_STEPS * g + min(n, QL_STEPS))
                        ge(pe, band_ready, NCH * g + max(0, k))
                    if n == 0:
                        pe.wait_ge(group_in, 2 * GH * 16 * (g + 1))
                    for q in tiles:
                        last = t.matmul(ql[:, q % QL_PER_STEP, :], q128[:, par, q // NT, (q % NT) * P:(q % NT + 1) * P], tabq[:],
                                        start=True, stop=True)
                    if tiles:
                        last.then_inc(ql_done, 1)
                    if 0 <= k < NCH:
                        for a in range(RQ_W):
                            w = RQ_W * k + a
                            keys = k128[:, par].rearrange("k h (t c) -> k h t c", c=P)[:, :, w // P:w // P + NT, w % P]
                            last = t.matmul(pk[:, a * GH * NT:(a + 1) * GH * NT], tabk[:, w // P, WIN - w:WIN - w + P], keys,
                                            start=True, stop=True)
                        last.then_inc(rq_done, 1)

                def main(g, n, par, end):
                    if n < ST:
                        j, row = n // NT, n % NT
                        if row == 0:
                            pe.wait_ge(head_in[j % 2], 32 * (2 * g + j // 2 + 1))
                        ge(pe, prob_ready, ST * g + n - 1)
                        split = row * P + PAD
                        for a, z in ((0, min(split, 512)), (512, split), (split, 512), (max(split, 512), S)):
                            if z > a:
                                base0 = a >= split
                                q = q0[:, j % 2, :] if base0 else q128[0:KR, par, j, :]
                                keys = k0[:, j % 2, a:z] if base0 else k128[:, par, j, PAD + a:PAD + z]
                                last = t.matmul(lg[n % 2][:, a:z], q[:, row * P:(row + 1) * P], keys, start=True, stop=True)
                        last.then_inc(lg_done, 1)
                    k = lag(g, n, LT)
                    if k is not None:
                        pe.wait_ge(prob_ready, ST * g + k + 1)
                        for half in range(2):
                            ge(pe, tp_read, 2 * (ST * g + k) + half - 1)
                            if half == 0:
                                ge(pe, near_read, ST * g + k - 2)
                            for a in range(4):
                                c0 = PAD + (4 * half + a) * P
                                last = t.transpose(tp[half][:, a * P:(a + 1) * P], prob[:, k % NR, c0:c0 + P], ident[:])
                            last.then_inc(tp_done, 1)
                    k = lag(g, n, LP)
                    if k is not None:
                        row, hd = k % NT, k // NT
                        if row == 0:
                            ge(pe, out_ready, GH * g + hd)
                            pe.wait_ge(val_in[hd % 2], 16 * (2 * g + hd // 2 + 1))
                        pe.wait_ge(tp_read, 2 * (ST * g + k + 1))
                        for a in range(NT):
                            t.matmul(o[:, row, :], probT[:, k % NR, a, :], vals[:, hd % 2, a, 0 if a <= row - 2 else 1, :],
                                     start=a == 0, stop=False)
                        pe.wait_ge(far_ready, ST * g + k + 1)
                        t.matmul(o[:, row, :], far[:, k % NR, :], tabv[:, 1, :], start=False, stop=False)
                        pe.wait_ge(near_read, ST * g + k + 1)
                        t.matmul(o[:, row, :], nearT[:, k % 2, :], tabv[:, 0, :], start=False, stop=True).then_inc(pv_done, 1)
                    k = lag(g, n, LU)
                    if k is not None:
                        pe.wait_ge(near_in[k % NR], 16 * (ST // NR * g + k // NR + 1))
                        pe.wait_ge(tp_read, 2 * (ST * g + min(n - LT, ST - 1)) + 1)
                        t.transpose(tp[0][:, 0:P], near[:, k % NR, :], ident[:]).then_inc(near_done, 1)

                pe.wait_ge(consts, 16 * len(const_loads))
                pe.wait_ge(cleared, 1)
                over_groups(pe, main, prefetch)

            @block.scalar
            def _(act):
                a = nc.scalar

                def main(g, n, par, end):
                    k = lag(g, n, LT)
                    if k is not None:
                        ge(act, pv_done, ST * g + k - NR + 1)
                        for half in range(2):
                            act.wait_ge(tp_done, 2 * (ST * g + k) + half + 1)
                            a.copy(probT[:, k % NR, 4 * half:4 * half + 4, :].rearrange("p a c -> p (a c)"),
                                   tp[half][:]).then_inc(tp_read, 1)
                    if n < ST:
                        ge(act, tp_done, 2 * (ST * g + n - NR + 1))
                        ge(act, win_out[n % NR], 16 * (ST // NR * g + n // NR))
                        act.wait_ge(max_ready, ST * g + n + 1)
                        a.activation(prob[:, n % NR, PAD:PAD + S], lg[n % 2][:], ACT.Exp,
                                     bias=nmax[:, n % NR:n % NR + 1]).then_inc(prob_ready, 1)
                    k = lag(g, n, LU)
                    if k is not None:
                        ge(act, pv_done, ST * g + k - 1)
                        act.wait_ge(near_done, ST * g + k + 1)
                        a.copy(nearT[:, k % 2, :], tp[0][:, 0:P]).then_inc(near_read, 1)

                act.wait_ge(cleared, 1)
                over_groups(act, main, lambda g, n, par: None)

            @block.gpsimd
            def _(pool):
                p = nc.gpsimd

                def main(g, n, par, end):
                    k = lag(g, n, LT)
                    if k is not None:
                        row, slot = k % NT, k % NR
                        ge(pool, pv_done, ST * g + k - NR + 1)
                        pool.wait_ge(tp_read, 2 * (ST * g + k + 1))
                        if row == 0:
                            p.tensor_tensor(far[:, slot, :], probT[:, slot, 0, :], fmask[:, 1, :], ALU.mult).then_inc(far_ready, 1)
                        else:
                            ge(pool, far_ready, ST * g + k)
                            p.tensor_tensor(farm[:], probT[:, slot, row - 1:row + 1, :], fmask[:], ALU.mult)
                            pool.drain()
                            p.tensor_tensor(far[:, slot, :], farm[:, 0, :], farm[:, 1, :], ALU.add).then_inc(far_ready, 1)

                pool.wait_ge(consts, 16 * len(const_loads))
                over_groups(pool, main, lambda g, n, par: None)

            @block.vector
            def _(dve):
                v = nc.vector

                def prefetch(g, n, par):
                    tiles = range(QL_PER_STEP * n, min(ST, QL_PER_STEP * (n + 1)))
                    if tiles:
                        dve.wait_ge(ql_done, QL_STEPS * g + n + 1)
                    for q in tiles:
                        j, row = q // NT, q % NT
                        if row == 0:
                            ge(dve, skew_out[(j - 2) % GH], 16 * (g + 1) if j >= 2 else 16 * g)
                        ins = v.scalar_tensor_tensor(qlin[:, j % 2, row, :], qmask[:], ql[:, q % QL_PER_STEP, P:P + 1],
                                                     ql[:, q % QL_PER_STEP, 0:P], ALU.mult, ALU.add)
                    if tiles:
                        ins.then_inc(ql_ready, 1)
                    k = n - RQ_FROM
                    if 0 <= k < NCH:
                        if k == 0:
                            dve.wait_ge(skew_in, 16 * 4 * GH * (g + 1))
                        dve.wait_ge(rq_done, NCH * g + k + 1)
                        dst = band[:, par].rearrange("p h t w -> p (h t) w")[:, :, RQ_W * k:RQ_W * (k + 1)]
                        v.tensor_tensor(dst, pk[:].rearrange("p (w n) -> p n w", w=RQ_W), dst, ALU.add).then_inc(band_ready, 1)

                def main(g, n, par, end):
                    if n < ST:
                        if n == 0:
                            dve.wait_ge(band_ready, NCH * (g + 1))
                        a, z, at = window(n % NT)
                        dve.wait_ge(lg_done, ST * g + n + 1)
                        v.tensor_tensor(lg[n % 2][:, a:z], lg[n % 2][:, a:z],
                                        band[:, par, n // NT, n % NT, at:at + z - a], ALU.add).then_inc(lg_added, 1)
                        dve.wait_ge(lg_added, ST * g + n + 1)
                        v.tensor_reduce(nmax[:, n % NR:n % NR + 1], lg[n % 2][:], AX.X, ALU.max, negate=True).then_inc(max_ready, 1)
                    k = lag(g, n, LP)
                    if k is not None and k % NT == NT - 1:
                        hd = k // NT
                        dve.wait_ge(pv_done, ST * g + k + 1)
                        ge(dve, out_stored[hd % 2], 16 * (2 * g + hd // 2))
                        v.reciprocal(rz[:, hd % 2, :], o[:, :, HD])
                        dve.drain()
                        v.tensor_tensor(out[:, hd % 2], o[:, :, 0:HD],
                                        rz[:, hd % 2].rearrange("p (t a) -> p t a", a=1).to_broadcast([P, NT, HD]),
                                        ALU.mult).then_inc(out_ready, 1)

                v.memset(k128[:], 0.0)
                v.memset(q128[:], 1.0)
                v.memset(prob[:], 0.0)
                v.memset(band[:], 0.0)
                dve.drain()
                dve.sem_inc(cleared, 1)
                dve.wait_ge(consts, 16 * len(const_loads))
                over_groups(dve, main, prefetch)


def combine_phase(nc, sem, i, scr, y):
    with ExitStack() as ctx:
        sb = lambda n, s, d=F32: ctx.enter_context(nc.sbuf_tensor(n, s, d))
        eo, xt, at = (sb(f"c_{n}", [P, 2, NT * D]) for n in ("eo", "x", "at"))
        pos, prob = sb("c_pos", [P, 2, NT * E]), sb("c_prob", [P, 2, NT * E])
        iota_c, ident = sb("c_iota_c", [P, CAP]), sb("c_ident", [P, P])
        comb, combT = sb("c_comb", [P, 2, E, CAP]), sb("c_combT", [P, 2, E, P])
        base, res = sb("c_base", [P, 2, NT, D]), sb("c_res", [P, 2, NT, D])
        tp = [ctx.enter_context(nc.psum_tensor(f"c_tp{n}", [P, 512], F32)) for n in range(4)]
        po = [ctx.enter_context(nc.psum_tensor(f"c_po{n}", [P, 512], F32)) for n in range(2)]
        consts = sem("c_consts")
        b_in = [sem("c_in0"), sem("c_in1")]
        base_ready, comb_ready, tp_done, tp_read, o_done, res_ready = (
            sem(f"c_{n}") for n in ("baser", "combr", "tpd", "tpr", "od", "resr"))
        stored = sem("c_stored")

        with nc.Block() as block:
            @block.sync
            def _(sp):
                def load(b, s):
                    for dst, src in ((eo, scr.eout.rearrange("b c e d -> b c (e d)")), (pos, scr.pos), (prob, scr.prob)):
                        sp.dma_start(dst[:, s], src[b]).then_inc(b_in[s], 16)
                    for k in range(2):
                        sp.dma_start(xt[:, s, k * NT * D // 2:(k + 1) * NT * D // 2].rearrange("p (t d) -> p t d", d=D),
                                     i["x"].rearrange("b (k t p) d -> b k p t d", k=2, p=P)[b, k]).then_inc(b_in[s], 16)
                        sp.dma_start(at[:, s, k * NT * D // 2:(k + 1) * NT * D // 2].rearrange("p (h n) -> p h n", h=H // 2),
                                     scr.attn.rearrange("(b k h) p n -> b k p h n", b=B, k=2)[b, k]).then_inc(b_in[s], 16)

                sp.dma_start(iota_c[:], i["iota_c"]).then_inc(consts, 16)
                sp.dma_start(ident[:], i["ident"]).then_inc(consts, 16)
                load(0, 0)
                load(1, 1)
                def store(b, s):
                    sp.wait_ge(res_ready, NT * (b + 1))
                    sp.dma_start(y.rearrange("b (t p) d -> b p t d", p=P)[b], res[:, s]).then_inc(stored, 16)

                def body(pair):
                    for s in range(2):
                        store(2 * pair + s, s)
                        load(2 * pair + s + 2, s)

                turns(sp, B // 2 - 1, body)
                store(B - 2, 0)
                store(B - 1, 1)
                sp.wait_ge(stored, 16 * B)

            @block.tensor
            def _(pe):
                t = nc.tensor
                pe.wait_ge(consts, 32)
                def body(pair):
                    for s in range(2):
                        b = 2 * pair + s
                        ge(pe, b_in[s], 112 * (pair + 1))
                        for n in range(NT):
                            ge(pe, comb_ready, NT * b + n + 1)
                            for half in range(2):
                                bank = tp[2 * (n % 2) + half]
                                if n >= 2:
                                    ge(pe, tp_read, 2 * (NT * b + n - 2) + half + 1)
                                for a in range(4):
                                    last = t.transpose(bank[:, a * P:(a + 1) * P], comb[:, n % 2, 4 * half + a, :], ident[:])
                                last.then_inc(tp_done, 1)
                            ge(pe, tp_read, 2 * (NT * b + n + 1))
                            ge(pe, res_ready, NT * b + max(0, n - 1))
                            for e in range(E):
                                last = t.matmul(po[n % 2][:, 0:D], combT[:, n % 2, e, :], eo[:, s, e * D:(e + 1) * D],
                                                start=e == 0, stop=e == E - 1)
                            last.then_inc(o_done, 1)

                turns(pe, B // 2, body)

            @block.scalar
            def _(act):
                def body(b):
                    for n in range(NT):
                        for half in range(2):
                            ge(act, tp_done, 2 * (NT * b + n) + half + 1)
                            if half == 0:
                                ge(act, o_done, NT * b + max(0, n - 1))
                            nc.scalar.copy(combT[:, n % 2, 4 * half:4 * half + 4, :].rearrange("p a c -> p (a c)"),
                                           tp[2 * (n % 2) + half][:]).then_inc(tp_read, 1)

                turns(act, B, body)

            @block.vector
            def _(dve):
                v = nc.vector
                dve.wait_ge(consts, 32)
                def body(pair):
                    for s in range(2):
                        b = 2 * pair + s
                        ge(dve, b_in[s], 112 * (pair + 1))
                        ge(dve, stored, 16 * b)
                        v.tensor_tensor(base[:, s].rearrange("p t (h d) -> p t h d", h=H),
                                        xt[:, s].rearrange("p (t h d) -> p t h d", t=NT, h=H),
                                        at[:, s].rearrange("p (h t d) -> p t h d", h=H, t=NT), ALU.add)
                        dve.drain()

                        def spread(n):
                            ge(dve, tp_done, 2 * (NT * b + max(0, n - 1)))
                            for e in range(E):
                                k = n * E + e
                                ins = v.tensor_scalar(comb[:, n % 2, e, :], iota_c[:], pos[:, s, k:k + 1],
                                                      prob[:, s, k:k + 1], ALU.is_equal, ALU.mult)
                            ins.then_inc(comb_ready, 1)

                        spread(0)
                        for n in range(NT):
                            if n + 1 < NT:
                                spread(n + 1)
                            ge(dve, o_done, NT * b + n + 1)
                            v.tensor_tensor(res[:, s, n, :], po[n % 2][:, 0:D], base[:, s, n, :], ALU.add).then_inc(res_ready, 1)

                turns(dve, B // 2, body)


def build(nc, ins, y, upto=5):
    with ExitStack() as ctx:
        sem = lambda name: ctx.enter_context(nc.semaphore(name))
        scr = Scratch(nc)
        tables_phase(nc, sem, ins, scr)
        tokens_phase(nc, sem, ins, scr)
        if upto > 2:
            experts_phase(nc, sem, ins, scr)
        if upto > 3:
            attend_phase(nc, sem, ins, scr)
        if upto > 4:
            combine_phase(nc, sem, ins, scr, y)


def layouts(x, Wq, Wk, Wv, Eq, Ek, Ev, wr, wi, wo):
    f = lambda a: np.ascontiguousarray(np.asarray(a))
    Eq, Ek, Ev = f(Eq), f(Ek), f(Ev)
    N = 2 * MAXD
    rev = N - np.arange(P + 1)
    clipped = np.clip(np.arange(3 * P) - P, 0, N)
    head_rows = lambda a: np.tile(a, H)
    marks = np.zeros((KR, 6), np.float32)
    for r in range(KR):
        marks[r, Q_SLOTS[r // HD]] = 1
        marks[r, 3 + K_SLOTS[r // HD]] = 1
    p, c = np.arange(P)[:, None], np.arange(P)[None, :]
    fmask = np.stack([c + MAXD > p, c - MAXD > p], 1).astype(np.float32)
    return {
        "x": f(x), "wq": f(Wq), "wk": f(Wk), "wv": f(Wv), "wr": f(wr), "wi": f(wi), "wo": f(wo),
        "ekx": f(np.tile(Ek[rev].T, (SLOTS, 1))), "eqx": f(np.tile(Eq[rev].T, (SLOTS, 1))),
        "equ": f(np.tile(Eq[clipped].T, (SLOTS, 1))),
        "eqk_cols": f(np.stack([np.tile(a, P // HD) for a in (Eq[N], Eq[0], Ek[N], Ek[0])], 1)),
        "evx": f(Ev[rev[:P]]),
        "ev_rows": f(np.broadcast_to(np.stack([head_rows(Ev[N]), head_rows(Ev[0])])[None], (P, 2, D))),
        "marks": marks,
        "ident": np.eye(P, dtype=np.float32),
        "iota_c": f(np.broadcast_to(np.arange(CAP, dtype=np.float32), (P, CAP))),
        "iota_e": f(np.broadcast_to(np.tile(np.arange(E, dtype=np.float32), NT), (P, NT * E))),
        "upper": f(np.concatenate([(p <= c), np.ones((P, P))], 1).astype(np.float32)),
        "qmask": (p + c >= P).astype(np.float32),
        "fmask": f(fmask),
    }


def program(arrays, nc, upto=5):
    ins = {n: nc.dram_tensor(f"in_{n}", a.shape, mybir.dt.from_np(a.dtype), kind="ExternalInput").ap()
           for n, a in arrays.items()}
    y = nc.dram_tensor("out_y", (B, S, D), F32, kind="ExternalOutput").ap()
    build(nc, ins, y, upto)


def kernel(**inputs):
    import concourse.bacc as bacc
    from concourse.bass_utils import run_bass_kernel_spmd

    names = ["L0_attn_x", "L0_attn_Wq", "L0_attn_Wk", "L0_attn_Wv", "L0_attn_Eq", "L0_attn_Ek", "L0_attn_Ev",
             "L0_ffn_w_router", "L0_ffn_wi", "L0_ffn_wo"]
    arrays = layouts(*[inputs[n] for n in names])
    nc = bacc.Bacc("TRN2", target_bir_lowering=False, num_devices=1)
    program(arrays, nc)
    got = run_bass_kernel_spmd(nc, [{f"in_{n}": a for n, a in arrays.items()}], core_ids=[0])
    return got.results[0]["out_y"]
```

```python
from contextlib import ExitStack

import concourse.bass as bass
import concourse.mybir as mybir
import numpy as np

F32, BF16 = mybir.dt.float32, mybir.dt.bfloat16
ALU, ACT, AX = mybir.AluOpType, mybir.ActivationFunctionType, mybir.AxisListType

P = 128
B, S, D = 8, 1024, 256
H, HD = 16, 16
NT = S // P
DH = D // P
E, CAP, F = 8, 128, 1024
FT = F // P
MAXD = 64
NH = B * H
GH = 4
NG = NH // GH
SLOTS = 6
KR = SLOTS * HD
QR = KR + 3
VW = HD + 1
QD = 4
CG = P // QD
NQH = NT // QD
WIN = 2 * P
PAD = 64
SCALE = 1.0 / HD ** 0.5
EPS = 1e-5
Q_SLOTS = (0, 0, 0, 1, 1, 2)
K_SLOTS = (2, 0, 1, 0, 1, 0)
Q128, Q0, K128, K0 = range(4)


def ge(eng, s, value):
    if not (isinstance(value, int) and value <= 0):
        eng.wait_ge(s, value)


def turns(eng, n, body):
    body(0)
    with eng.Fori(1, n) as k:
        body(k)


def batch_pairs(eng, body):
    body(0, False)
    with eng.Fori(1, B // 2 - 1) as pair:
        body(pair, False)
    body(B // 2 - 1, True)


def dram(nc, name, shape, dt, kind="Internal"):
    return nc.dram_tensor(name, shape, dt, kind=kind).ap()


class Scratch:

    def __init__(self, nc):
        self.opnd = dram(nc, "opnd", (4, SLOTS, B, D, S), BF16)
        self.vals = dram(nc, "vals", (NH, P, NT, 2, VW), F32)
        self.pos = dram(nc, "pos", (B, P, NT * E), F32)
        self.prob = dram(nc, "prob", (B, P, NT * E), F32)
        self.ein = dram(nc, "ein", (E, DH, P, B, CAP), F32)
        self.eout = dram(nc, "eout", (B, CAP, E, D), F32)
        self.attn = dram(nc, "attn", (NH, NQH, P, P), F32)
        self.tabq = dram(nc, "tabq", (QR, P + 1), BF16)
        self.tabk = dram(nc, "tabk", (2, KR, 3 * P), BF16)
        self.tabv = dram(nc, "tabv", (2, P, VW), F32)
        self.skew = dram(nc, "skew", (4, P, NT, 2 * P), F32)
        self.prow = dram(nc, "prow", (8, P, WIN), F32)


def tokens_phase(nc, sem, i, scr):
    with ExitStack() as ctx:
        sb = lambda n, s, d=F32: ctx.enter_context(nc.sbuf_tensor(n, s, d))
        xt, xn = sb("a_x", [P, NT, D]), sb("a_xn", [P, 2, NT, D])
        xnT = sb("a_xnT", [P, DH, S])
        wq, wk, wv = (sb(f"a_{n}", [P, DH, D]) for n in ("wq", "wk", "wv"))
        wr = sb("a_wr", [P, DH, E])
        ident = sb("a_ident", [P, P])
        cols = sb("a_cols", [P, 4])
        evrow = sb("a_evrow", [P, 2, D])
        iota_c, iota_e = sb("a_iota_c", [P, CAP]), sb("a_iota_e", [P, NT * E])
        upper = sb("a_upper", [P, 2 * P])
        tri = sb("a_tri", [P, 2 * P], BF16)
        stats, mv = sb("a_stats", [P, NT, 6]), sb("a_mv", [P, NT, 2])
        std, rstd = sb("a_std", [P, NT]), sb("a_rstd", [P, NT])
        proj = sb("a_proj", [P, 2, 2, S])
        hi, mid, lo = (sb(f"a_{n}", [P, 4, 2, S], BF16) for n in ("hi", "mid", "lo"))
        rest = sb("a_rest", [P, 2, 2, S])
        vraw = sb("a_vraw", [P, NT, D])
        vb = sb("a_vb", [P, H, NT, 2, VW])
        lmax, lsub, lexp, prob = (sb(f"a_{n}", [P, NT, E]) for n in ("lmax", "lsub", "lexp", "prob"))
        red, rsum = sb("a_red", [P, NT]), sb("a_rsum", [P, NT])
        same, cand, left = (sb(f"a_{n}", [P, NT, E]) for n in ("same", "cand", "left"))
        pick = sb("a_pick", [P, 2, NT, E])
        pickb = sb("a_pickb", [P, 2 * NT, E], BF16)
        prk = sb("a_prk", [P, 2, NT * E])
        pos = sb("a_pos", [P, NT * E])
        disp = sb("a_disp", [P, 4, E * CAP], BF16)
        xh, xm, xl = (sb(f"a_{n}", [P, 2, NT, D], BF16) for n in ("xh", "xm", "xl"))
        xrest = sb("a_xrest", [P, NT, D])
        ein = sb("a_ein", [P, DH, E * CAP])
        ps = [ctx.enter_context(nc.psum_tensor(f"a_ps{n}", [P, 512], F32)) for n in range(8)]
        big = ps[0:4]
        pproj, tb, prt = ps[4:6], ps[4:7], ps[7]

        w_in, x_in = sem("a_w_in"), sem("a_x_in")
        carrier = sem("a_carrier")
        tri_ready, var_ready, std_ready, xn_ready = (sem(f"a_{n}") for n in ("tri", "var", "stdr", "xnr"))
        t_done, t_evac = sem("a_t_done"), sem("a_t_evac")
        lg_done, lsub_ready, exp_ready = (sem(f"a_{n}") for n in ("lg", "lsubr", "expr"))
        pick_ready, rank_done, pos_ready, pos_out = (sem(f"a_{n}") for n in ("pickr", "rank", "posr", "poso"))
        disp_ready, disp_used, in_done, in_evac, ein_out = (sem(f"a_{n}") for n in ("dispr", "dispu", "ind", "ine", "eino"))
        v_done, v_read, v_evac, vals_out = sem("a_v_done"), sem("a_v_read"), sem("a_v_evac"), sem("a_vals_out")
        vb_cleared = sem("a_vb_cleared")
        pr_done, proj_ready, hi_ready, rest_ready, mid_ready, lo_ready = (
            sem(f"a_{n}") for n in ("prd", "projr", "hir", "restr", "midr", "lor"))
        xh_ready, xrest_ready, xm_ready, xl_ready = (sem(f"a_{n}") for n in ("xhr", "xrestr", "xmr", "xlr"))
        parts_out = [sem(f"a_partso{n}") for n in range(4)]
        NL = 14
        units = [(w, op, h) for w, op in ((wq, Q128), (wk, K128)) for h in range(DH)]
        NUN = len(units)

        with nc.Block() as block:
            @block.sync
            def _(sp):
                loads = [(wq[:, h, :], i["wq"][h * P:(h + 1) * P, :]) for h in range(DH)]
                loads += [(wk[:, h, :], i["wk"][h * P:(h + 1) * P, :]) for h in range(DH)]
                loads += [(wv[:, h, :], i["wv"][h * P:(h + 1) * P, :]) for h in range(DH)]
                loads += [(wr[:, h, :], i["wr"][h * P:(h + 1) * P, :]) for h in range(DH)]
                loads += [(ident[:], i["ident"]), (cols[:], i["eqk_cols"]), (evrow[:], i["ev_rows"]),
                          (iota_c[:], i["iota_c"]), (iota_e[:], i["iota_e"]), (upper[:], i["upper"])]
                assert len(loads) == NL
                def load_x(b):
                    for k in range(2):
                        sp.dma_start(xt[:, 4 * k:4 * k + 4, :], i["x"][b, k * S // 2:(k + 1) * S // 2].rearrange(
                            "(t p) d -> p t d", p=P)).then_inc(x_in, 16)

                def body(pair, last):
                    for s in range(2):
                        b = 2 * pair + s
                        if not (last and s == 1):
                            ge(sp, xn_ready, b + 1)
                            load_x(b + 1)
                        ge(sp, v_evac, NT * (b + 1))
                        sp.sem_inc(carrier, 1)
                        sp.dma_start(scr.vals.rearrange("(b h) p t c n -> b p h (t c n)", b=B)[b],
                                     vb[:].rearrange("p h t c n -> p h (t c n)")).then_inc(vals_out, 16)
                        ge(sp, pos_ready, b + 1)
                        sp.sem_inc(carrier, 1)
                        sp.dma_start(scr.pos[b], pos[:]).then_inc(pos_out, 16)
                        sp.dma_start(scr.prob[b], prob[:].rearrange("p t e -> p (t e)")).then_inc(pos_out, 16)
                        for u, (_, op, h) in enumerate(units):
                            slots = Q_SLOTS if op == Q128 else K_SLOTS
                            for part, (src, ready) in enumerate(((hi, hi_ready), (mid, mid_ready), (lo, lo_ready))):
                                ge(sp, ready, NUN * b + u + 1)
                                sp.sem_inc(carrier, 1)
                                at = [s for s in range(SLOTS) if slots[s] == part]
                                step = at[1] - at[0] if len(at) > 1 else 1
                                for c in range(2):
                                    dst = scr.opnd[op + c].rearrange("s b e n -> b e s n")[b, h * P:(h + 1) * P]
                                    sp.dma_start(dst[:, at[0]:at[-1] + 1:step, :],
                                                 src[:, u, c:c + 1, :].to_broadcast([P, len(at), S])
                                                 ).then_inc(parts_out[u], 16)
                        ge(sp, in_evac, 4 * (b + 1))
                        sp.sem_inc(carrier, 1)
                        for h in range(DH):
                            sp.dma_start(scr.ein[:, h].rearrange("e p b c -> b p e c")[b],
                                         ein[:, h, :].rearrange("p (e c) -> p e c", e=E)).then_inc(ein_out, 16)

                load_x(0)
                for dst, src in loads:
                    sp.dma_start(dst, src).then_inc(w_in, 16)
                batch_pairs(sp, body)
                sp.wait_ge(pos_out, 32 * B)
                sp.wait_ge(vals_out, 16 * B)
                for k in range(NUN):
                    sp.wait_ge(parts_out[k], 96 * B)
                sp.wait_ge(ein_out, 32 * B)

            @block.tensor
            def _(pe):
                t = nc.tensor

                def transpose_x(b, s):
                    ge(pe, xn_ready, b + 1)
                    ge(pe, proj_ready, 2 * NUN * b)
                    for k in range(4):
                        if k == 3:
                            ge(pe, t_evac, 4 * b + 1)
                        for n in range(4):
                            last = t.transpose(tb[k % 3][:, n * P:(n + 1) * P],
                                               xn[:, s, 4 * (k % 2) + n, (k // 2) * P:(k // 2 + 1) * P], ident[:])
                        last.then_inc(t_done, 1)

                def body(pair, last_pair):
                    for s in range(2):
                        b = 2 * pair + s
                        ge(pe, t_evac, 4 * (b + 1))
                        ge(pe, pos_ready, b)
                        for n in range(NT):
                            for h in range(DH):
                                last = t.matmul(prt[:, n * E:(n + 1) * E], xnT[:, h, n * P:(n + 1) * P], wr[:, h, :],
                                                start=h == 0, stop=h == DH - 1)
                        last.then_inc(lg_done, 1)
                        for n in range(NT):
                            if n >= 2:
                                ge(pe, v_read, NT * b + n - 1)
                            for h in range(DH):
                                last = t.matmul(pproj[n % 2][:, 0:D], xnT[:, h, n * P:(n + 1) * P], wv[:, h, :],
                                                start=h == 0, stop=h == DH - 1)
                            last.then_inc(v_done, 1)
                        for u, (w, _, eh) in enumerate(units):
                            if u == 0:
                                ge(pe, v_read, NT * (b + 1))
                            for half in range(2):
                                if u > 0:
                                    ge(pe, proj_ready, 2 * (NUN * b + u - 1) + half + 1)
                                for h in range(DH):
                                    last = t.matmul(pproj[half][:], w[:, h, eh * P:(eh + 1) * P],
                                                    xnT[:, h, half * 512:(half + 1) * 512], start=h == 0, stop=h == DH - 1)
                                last.then_inc(pr_done, 1)
                            if u == 0:
                                ge(pe, pick_ready, b + 1)
                                t.matmul(prt[:, 0:2 * NT * E], tri[:, 0:P], pickb[:].rearrange("p k e -> p (k e)"),
                                         start=True, stop=False)
                                for k in range(2 * NT - 1):
                                    n = 2 * NT - 1 - k
                                    last = t.matmul(prt[:, (k + 1) * E:2 * NT * E], tri[:, P:2 * P],
                                                    pickb[:, k:k + 1, :].to_broadcast([P, n, E]),
                                                    start=False, stop=k == 2 * NT - 2)
                                last.then_inc(rank_done, 1)
                        ge(pe, in_evac, 4 * b)
                        ge(pe, xl_ready, b + 1)
                        for n in range(NT):
                            if n == NT - 1 and not (last_pair and s == 1):
                                transpose_x(b + 1, 1 - s)
                            ge(pe, disp_ready, NT * b + n + 1)
                            for h in range(DH):
                                for part in (xh, xm, xl):
                                    for half in range(2):
                                        last = t.matmul(big[2 * h + half][:], part[:, s, n, h * P:(h + 1) * P],
                                                        disp[:, n % 4, half * 512:(half + 1) * 512],
                                                        start=n == 0 and part is xh, stop=n == NT - 1 and part is xl)
                            last.then_inc(disp_used, 1)

                pe.wait_ge(w_in, 16 * NL)
                pe.wait_ge(tri_ready, 1)
                transpose_x(0, 0)
                batch_pairs(pe, body)

            @block.scalar
            def _(act):
                a = nc.scalar

                def root(b):
                    ge(act, var_ready, b + 1)
                    a.activation(std[:], std[:], ACT.Sqrt).then_inc(std_ready, 1)

                def transposes(b, s):
                    for k in range(4):
                        ge(act, t_done, 4 * b + k + 1)
                        a.copy(xnT[:, k // 2, (k % 2) * 512:(k % 2 + 1) * 512], tb[k % 3][:]).then_inc(t_evac, 1)
                    ge(act, disp_used, NT * (b - 1))
                    a.copy(xh[:, s], xn[:, s]).then_inc(xh_ready, 1)

                def inputs(b):
                    ge(act, ein_out, 32 * b)
                    ge(act, disp_used, NT * (b + 1))
                    for k in range(4):
                        a.copy(ein[:, k // 2, (k % 2) * 512:(k % 2 + 1) * 512], big[k][:]).then_inc(in_evac, 1)

                def body(pair, last):
                    for s in range(2):
                        b = 2 * pair + s
                        ge(act, lsub_ready, b + 1)
                        a.activation(lexp[:], lsub[:], ACT.Exp).then_inc(exp_ready, 1)
                        ge(act, xrest_ready, b + 1)
                        a.copy(xm[:, s], xrest[:]).then_inc(xm_ready, 1)
                        ge(act, v_evac, NT * b)
                        for n in range(NT):
                            ge(act, v_done, NT * b + n + 1)
                            a.copy(vraw[:, n, :], pproj[n % 2][:, 0:D]).then_inc(v_read, 1)
                        if s == 1 or not isinstance(b, int) or b > 0:
                            inputs(b - 1)

                        def high(u):
                            ge(act, proj_ready, 2 * (NUN * b + u + 1))
                            ge(act, parts_out[u], 96 * b)
                            a.copy(hi[:, u], proj[:, u % 2]).then_inc(hi_ready, 1)

                        def middle(u):
                            ge(act, rest_ready, NUN * b + u + 1)
                            a.copy(mid[:, u], rest[:, u % 2]).then_inc(mid_ready, 1)

                        high(0)
                        for u in range(1, NUN):
                            high(u)
                            middle(u - 1)
                        if not (last and s == 1):
                            root(b + 1)
                        middle(NUN - 1)
                        if not (last and s == 1):
                            transposes(b + 1, 1 - s)

                root(0)
                transposes(0, 0)
                batch_pairs(act, body)
                inputs(B - 1)

            @block.gpsimd
            def _(pool):
                p = nc.gpsimd

                def body(pair, last):
                    for s in range(2):
                        b = 2 * pair + s
                        ge(pool, xl_ready, b)
                        ge(pool, xh_ready, b + 1)
                        p.tensor_tensor(xrest[:], xn[:, s], xh[:, s], ALU.subtract).then_inc(xrest_ready, 1)
                        ge(pool, xm_ready, b + 1)
                        p.tensor_tensor(xl[:, s], xrest[:], xm[:, s], ALU.subtract).then_inc(xl_ready, 1)
                        ge(pool, vals_out, 16 * b)
                        for n in range(NT):
                            ge(pool, v_read, NT * b + n + 1)
                            src = vraw[:, n, :].rearrange("p (h d) -> p h d", h=H)
                            for c in range(2):
                                ins = p.tensor_tensor(vb[:, :, n, c, 0:HD], src,
                                                      evrow[:, c, :].rearrange("p (h d) -> p h d", h=H), ALU.add)
                            ins.then_inc(v_evac, 1)
                        for u in range(NUN):
                            ge(pool, hi_ready, NUN * b + u + 1)
                            ge(pool, lo_ready, NUN * b + u - 1 if u >= 2 else NUN * b)
                            p.tensor_tensor(rest[:, u % 2], proj[:, u % 2], hi[:, u], ALU.subtract).then_inc(rest_ready, 1)

                pool.wait_ge(w_in, 16 * NL)
                pool.wait_ge(vb_cleared, 1)
                batch_pairs(pool, body)

            @block.vector
            def _(dve):
                v = nc.vector
                row = lambda ap: ap[:].rearrange("p (t a) -> p t a", a=1).to_broadcast([P, NT, E])
                ie = iota_e[:].rearrange("p (t e) -> p t e", e=E)

                def moments(b):
                    ge(dve, x_in, 32 * (b + 1))
                    for n in range(NT):
                        v.bn_stats(stats[:, n, :], xt[:, n, :])
                    dve.drain()
                    for n in range(NT):
                        v.bn_aggr(mv[:, n, :], stats[:, n, :])
                    dve.drain()
                    v.tensor_scalar(std[:], mv[:, :, 1], EPS, None, ALU.add).then_inc(var_ready, 1)

                def normalize(b, s):
                    ge(dve, std_ready, b + 1)
                    v.reciprocal(rstd[:], std[:])
                    dve.drain()
                    ge(dve, disp_used, NT * (b - 1))
                    for n in range(NT):
                        ins = v.tensor_scalar(xn[:, s, n, :], xt[:, n, :], mv[:, n, 0:1], rstd[:, n:n + 1],
                                              ALU.subtract, ALU.mult)
                    ins.then_inc(xn_ready, 1)

                def body(pair, last):
                    for s in range(2):
                        b = 2 * pair + s
                        ge(dve, lg_done, b + 1)
                        lg = prt[:, 0:NT * E].rearrange("p (t e) -> p t e", e=E)
                        v.tensor_reduce(red[:], lg, AX.X, ALU.max)
                        dve.drain()
                        v.tensor_tensor(lsub[:], lg, row(red), ALU.subtract).then_inc(lsub_ready, 1)
                        ge(dve, exp_ready, b + 1)
                        v.tensor_reduce(rsum[:], lexp[:], AX.X, ALU.add)
                        dve.drain()
                        v.reciprocal(rsum[:], rsum[:])
                        dve.drain()
                        ge(dve, pos_out, 32 * b)
                        v.tensor_tensor(prob[:], lexp[:], row(rsum), ALU.mult)
                        dve.drain()
                        for k in range(2):
                            src = prob if k == 0 else left
                            v.tensor_reduce(red[:], src[:], AX.X, ALU.max)
                            dve.drain()
                            v.tensor_tensor(same[:], src[:], row(red), ALU.is_equal)
                            dve.drain()
                            v.scalar_tensor_tensor(cand[:], same[:], -float(E), ie, ALU.mult, ALU.add)
                            dve.drain()
                            v.tensor_reduce(red[:], cand[:], AX.X, ALU.min)
                            dve.drain()
                            v.tensor_scalar(red[:], red[:], float(E), None, ALU.add)
                            dve.drain()
                            v.tensor_tensor(pick[:, k], ie, row(red), ALU.is_equal)
                            dve.drain()
                            if k == 0:
                                v.scalar_tensor_tensor(left[:], pick[:, 0], -4.0, prob[:], ALU.mult, ALU.add)
                                dve.drain()
                        v.tensor_copy(pickb[:], pick[:].rearrange("p k t e -> p (k t) e")).then_inc(pick_ready, 1)

                        def project(u):
                            ge(dve, rest_ready, NUN * b + u - 1 if u >= 2 else NUN * b)
                            op = units[u][1]
                            for half in range(2):
                                ge(dve, pr_done, 2 * (NUN * b + u) + half + 1)
                                for c in range(2):
                                    dst = proj[:, u % 2, c, half * 512:(half + 1) * 512]
                                    if op == Q128:
                                        ins = v.tensor_scalar(dst, pproj[half][:], cols[:, c:c + 1], SCALE, ALU.add, ALU.mult)
                                    else:
                                        ins = v.tensor_scalar(dst, pproj[half][:], cols[:, 2 + c:3 + c], None, ALU.add)
                                ins.then_inc(proj_ready, 1)

                        def low(u):
                            ge(dve, mid_ready, NUN * b + u + 1)
                            ge(dve, parts_out[u], 96 * b)
                            v.tensor_tensor(lo[:, u], rest[:, u % 2], mid[:, u], ALU.subtract).then_inc(lo_ready, 1)

                        def one_hot(n):
                            ge(dve, disp_used, NT * b + n - 3)
                            for e in range(E):
                                ins = v.tensor_scalar(disp[:, n % 4, e * CAP:(e + 1) * CAP], iota_c[:],
                                                      pos[:, n * E + e:n * E + e + 1], None, ALU.is_equal)
                            ins.then_inc(disp_ready, 1)

                        project(0)
                        ge(dve, rank_done, b + 1)
                        v.tensor_tensor(prk[:].rearrange("p k n -> p (k n)"), prt[:, 0:2 * NT * E],
                                        pick[:].rearrange("p k t e -> p (k t e)"), ALU.mult)
                        dve.drain()
                        v.scalar_tensor_tensor(pos[:], prk[:, 0, :], -1.0, prk[:, 1, :], ALU.add, ALU.add).then_inc(pos_ready, 1)
                        dve.drain()
                        one_hot(0)
                        project(1)
                        one_hot(1)
                        project(2)
                        low(0)
                        one_hot(2)
                        project(3)
                        low(1)
                        one_hot(3)
                        more = not (last and s == 1)
                        one_hot(4)
                        if more:
                            moments(b + 1)
                        low(2)
                        one_hot(5)
                        if more:
                            normalize(b + 1, 1 - s)
                        one_hot(6)
                        low(3)
                        one_hot(7)

                v.memset(vb[:], 1.0).then_inc(vb_cleared, 1)
                moments(0)
                normalize(0, 0)
                dve.wait_ge(w_in, 16 * NL)
                v.tensor_copy(tri[:], upper[:]).then_inc(tri_ready, 1)
                batch_pairs(dve, body)


def tables_programs(nc, sem, i, scr, ctx, pc):
    sb = lambda n, s, d=F32: ctx.enter_context(nc.sbuf_tensor(n, s, d))
    NX, NU = P + 1, 3 * P
    ekx, eqx = sb("t_ekx", [KR, NX]), sb("t_eqx", [KR, NX])
    equ = sb("t_equ", [KR, NU])
    cols = sb("t_cols", [KR, 4])
    evx, ev128, ev0 = sb("t_evx", [P, HD]), sb("t_ev128", [P, HD]), sb("t_ev0", [P, HD])
    marks = sb("t_marks", [KR, 6])
    tq = sb("t_tq", [KR, NX])
    prod = sb("t_prod", [KR, NX])
    diff = sb("t_diff", [KR, 2])
    negd = sb("t_negd", [KR, 1])
    ones = sb("t_ones", [KR, 1])
    tk = sb("t_tk", [KR, 2, NU])
    hi, mid, lo = (sb(f"t_{n}", [KR, 2 * NU], BF16) for n in ("hi", "mid", "lo"))
    rest, mix = sb("t_rest", [KR, 2 * NU]), sb("t_mix", [KR, 2 * NU])
    outq, outk = sb("t_outq", [KR, NX], BF16), sb("t_outk", [KR, 2 * NU], BF16)
    crow, crest = sb("t_crow", [1, NX]), sb("t_crest", [1, NX])
    cpart = sb("t_cpart", [1, 3, NX], BF16)
    tv = sb("t_tv", [P, 2, VW])
    zero = sb("t_zero", [P, NT * 2 * P])
    loaded, zeroed, prod_ready, const_ready, const_read = (
        sem(f"t_{n}") for n in ("loaded", "zeroed", "prod", "const", "constrd"))
    tables_ready, stored = sem("t_ready"), sem("t_stored")

    def load(sp):
        for dst, src in ((ekx, i["ekx"]), (eqx, i["eqx"]), (equ, i["equ"]), (cols, i["eqk_cols"][0:KR]),
                         (evx, i["evx"]), (ev128, i["ev_rows"][:, 0, 0:HD]), (ev0, i["ev_rows"][:, 1, 0:HD]),
                         (marks, i["marks"])):
            sp.dma_start(dst[:], src).then_inc(loaded, 16)

    def store(sp):
        sp.wait_ge(zeroed, 1)
        for n in range(4):
            sp.dma_start(scr.skew[n].rearrange("p t n -> p (t n)"), zero[:]).then_inc(stored, 16)
        sp.wait_ge(tables_ready, 1)
        sp.dma_start(scr.tabq[0:KR, :], outq[:]).then_inc(stored, 16)
        sp.dma_start(scr.tabq[KR:QR, :].rearrange("(a r) n -> a r n", a=1), cpart[:]).then_inc(stored, 16)
        sp.dma_start(scr.tabk.rearrange("c k n -> k c n"), outk[:].rearrange("k (c n) -> k c n", c=2)).then_inc(stored, 16)
        sp.dma_start(scr.tabv.rearrange("c p n -> p c n"), tv[:]).then_inc(stored, 16)
        sp.wait_ge(stored, 16 * 8)

    def tensor(pe):
        pe.wait_ge(prod_ready, 1)
        nc.tensor.matmul(pc[0:1, 0:NX], ones[0:HD, :], prod[0:HD, :], start=True, stop=True).then_inc(const_ready, 1)
        pe.wait_ge(const_read, 1)

    def gpsimd(pool):
        nc.gpsimd.memset(zero[:], 0.0).then_inc(zeroed, 1)

    def vector(dve):
        v = nc.vector
        v.memset(ones[:], 1.0)
        v.memset(tv[:], 0.0)
        dve.wait_ge(loaded, 16 * 8)
        dve.drain()
        v.tensor_tensor(diff[:, 0:1], cols[:, 0:1], cols[:, 1:2], ALU.subtract)
        v.tensor_tensor(diff[:, 1:2], cols[:, 2:3], cols[:, 3:4], ALU.subtract)
        v.tensor_scalar(tq[:, 0:P], ekx[:, 0:P], cols[:, 2:3], None, ALU.subtract)
        v.tensor_scalar(prod[:, 0:P], eqx[:, 0:P], cols[:, 0:1], SCALE, ALU.subtract, ALU.mult)
        v.tensor_scalar(tk[:, 0, :], equ[:], cols[:, 0:1], SCALE, ALU.subtract, ALU.mult)
        v.tensor_scalar(tk[:, 1, :], equ[:], cols[:, 1:2], SCALE, ALU.subtract, ALU.mult)
        dve.drain()
        v.tensor_copy(tq[:, P:NX], diff[:, 1:2])
        v.tensor_scalar(negd[:], diff[:, 0:1], -SCALE, None, ALU.mult)
        v.tensor_tensor(tv[:, 0, 0:HD], evx[:], ev0[:], ALU.subtract)
        v.tensor_tensor(tv[:, 1, 0:HD], ev128[:], ev0[:], ALU.subtract)
        dve.drain()
        v.tensor_tensor(prod[:, 0:P], prod[:, 0:P], tq[:, 0:P], ALU.mult)
        v.tensor_tensor(prod[:, P:NX], negd[:], diff[:, 1:2], ALU.mult).then_inc(prod_ready, 1)

        dve.wait_ge(const_ready, 1)
        v.tensor_copy(crow[:], pc[0:1, 0:NX]).then_inc(const_read, 1)

        def split(src, n, marks3, out):
            dve.drain()
            v.tensor_copy(hi[:, 0:n], src)
            dve.drain()
            v.tensor_tensor(rest[:, 0:n], src, hi[:, 0:n], ALU.subtract)
            dve.drain()
            v.tensor_copy(mid[:, 0:n], rest[:, 0:n])
            dve.drain()
            v.tensor_tensor(lo[:, 0:n], rest[:, 0:n], mid[:, 0:n], ALU.subtract)
            v.tensor_scalar(mix[:, 0:n], hi[:, 0:n], marks3[:, 0:1], None, ALU.mult)
            dve.drain()
            v.scalar_tensor_tensor(rest[:, 0:n], mid[:, 0:n], marks3[:, 1:2], mix[:, 0:n], ALU.mult, ALU.add)
            dve.drain()
            v.scalar_tensor_tensor(out, lo[:, 0:n], marks3[:, 2:3], rest[:, 0:n], ALU.mult, ALU.add)

        split(tq[:], NX, marks[:, 3:6], outq[:])
        split(tk[:].rearrange("k c n -> k (c n)"), 2 * NU, marks[:, 0:3], outk[:])
        dve.drain()
        v.tensor_copy(cpart[:, 0, :], crow[:])
        dve.drain()
        v.tensor_tensor(crest[:], crow[:], cpart[:, 0, :], ALU.subtract)
        dve.drain()
        v.tensor_copy(cpart[:, 1, :], crest[:])
        dve.drain()
        v.tensor_tensor(cpart[:, 2, :], crest[:], cpart[:, 1, :], ALU.subtract)
        dve.drain()
        dve.sem_inc(tables_ready, 1)

    return load, store, tensor, gpsimd, vector


def experts_phase(nc, sem, i, scr):
    GC = B * CAP
    with ExitStack() as ctx:
        sb = lambda n, s, d=F32: ctx.enter_context(nc.sbuf_tensor(n, s, d))
        wi = [sb(f"e_wi{n}", [P, DH, F]) for n in range(2)]
        wo = [sb(f"e_wo{n}", [P, FT, D]) for n in range(2)]
        xin = [sb(f"e_xin{n}", [P, DH, GC]) for n in range(2)]
        hid = sb("e_hid", [P, FT, GC])
        res = sb("e_res", [P, B, D])
        ph = [ctx.enter_context(nc.psum_tensor(f"e_ph{n}", [P, 512], F32)) for n in range(4)]
        po = [ctx.enter_context(nc.psum_tensor(f"e_po{n}", [P, 512], F32)) for n in range(4)]
        e_in = [sem("e_in0"), sem("e_in1")]
        h_done, h_ready, o_done, o_ready, res_out = (sem(f"e_{n}") for n in ("hd", "hr", "od", "or", "ro"))
        load_tables, store_tables, tables_tensor, tables_gpsimd, tables_vector = tables_programs(
            nc, sem, i, scr, ctx, po[0])
        UH, UO = 2 * FT, B

        with nc.Block() as block:
            @block.sync
            def _(sp):
                def load(e, s):
                    for h in range(DH):
                        sp.dma_start(wi[s][:, h, :], i["wi"][e, h * P:(h + 1) * P, :]).then_inc(e_in[s], 16)
                        sp.dma_start(xin[s][:, h, :], scr.ein[e, h].rearrange("p b c -> p (b c)")).then_inc(e_in[s], 16)
                    for k in range(2):
                        sp.dma_start(wo[s][:, 4 * k:4 * k + 4, :], i["wo"][e, k * F // 2:(k + 1) * F // 2].rearrange(
                            "(t p) d -> p t d", p=P)).then_inc(e_in[s], 16)

                load_tables(sp)
                load(0, 0)
                load(1, 1)
                store_tables(sp)
                def store(e):
                    ge(sp, o_ready, UO * (e + 1))
                    sp.dma_start(scr.eout.rearrange("b c e d -> e c b d")[e], res[:]).then_inc(res_out, 16)

                def body(pair):
                    for s in range(2):
                        store(2 * pair + s)
                        load(2 * pair + s + 2, s)

                turns(sp, E // 2 - 1, body)
                store(E - 2)
                store(E - 1)
                sp.wait_ge(res_out, 16 * E)

            @block.tensor
            def _(pe):
                t = nc.tensor
                tables_tensor(pe)

                def body(pair):
                    for s in range(2):
                        e = 2 * pair + s
                        ge(pe, e_in[s], 96 * (pair + 1))
                        for f in range(FT):
                            for half in range(2):
                                k = 2 * f + half
                                if k >= 4:
                                    ge(pe, h_ready, UH * e + k - 3)
                                for h in range(DH):
                                    last = t.matmul(ph[k % 4][:], wi[s][:, h, f * P:(f + 1) * P],
                                                    xin[s][:, h, half * 512:(half + 1) * 512],
                                                    start=h == 0, stop=h == DH - 1)
                                last.then_inc(h_done, 1)
                        ge(pe, h_ready, UH * (e + 1))
                        for g in range(B):
                            ge(pe, o_ready, UO * e + max(0, g - 3))
                            for f in range(FT):
                                last = t.matmul(po[g % 4][:, 0:D], hid[:, f, g * CAP:(g + 1) * CAP], wo[s][:, f, :],
                                                start=f == 0, stop=f == FT - 1)
                            last.then_inc(o_done, 1)

                turns(pe, E // 2, body)

            @block.scalar
            def _(act):
                def body(e):
                    ge(act, o_done, UO * e)
                    for k in range(UH):
                        ge(act, h_done, UH * e + k + 1)
                        nc.scalar.activation(hid[:, k // 2, (k % 2) * 512:(k % 2 + 1) * 512], ph[k % 4][:],
                                             ACT.Gelu_apprx_tanh).then_inc(h_ready, 1)

                turns(act, E, body)

            @block.gpsimd
            def _(pool):
                tables_gpsimd(pool)

            @block.vector
            def _(dve):
                tables_vector(dve)

                def body(e):
                    ge(dve, res_out, 16 * e)
                    for g in range(B):
                        ge(dve, o_done, UO * e + g + 1)
                        nc.vector.tensor_copy(res[:, g, :], po[g % 4][:, 0:D]).then_inc(o_ready, 1)

                turns(dve, E, body)


LE, LT, LU, LP = 1, 3, 6, 7
NR = 4
NP = 2 * QD
ST = GH * NT
NQ = ST // QD
END = ST + LP + 1
QUAD_STEPS = ((0, 1), (2, 3, "far"), (4, 5, 6), (7, "near"))
QL_PER_STEP = 3
QL_STEPS = -(-ST // QL_PER_STEP)
QL_FROM, RQ_FROM = 1, 16
RQ_W = 16
NCH = WIN // RQ_W


def attend_phase(nc, sem, i, scr):
    with ExitStack() as ctx:
        sb = lambda n, s, d=F32: ctx.enter_context(nc.sbuf_tensor(n, s, d))
        k128 = sb("d_k128", [KR, 2, GH, S + 2 * PAD], BF16)
        q128 = sb("d_q128", [QR, 2, GH, S], BF16)
        k0, q0 = sb("d_k0", [KR, 2, S], BF16), sb("d_q0", [KR, 2, S], BF16)
        vals = sb("d_vals", [P, 2, NT, 2, VW])
        band = sb("d_band", [P, 2, GH, NT, WIN])
        qlin = sb("d_qlin", [P, GH, NT, P])
        prob = sb("d_prob", [P, NR, S + 2 * PAD])
        probT = sb("d_probT", [P, NP, NT, P])
        farm, far = sb("d_farm", [P, 2, P]), sb("d_far", [P, NP, P])
        near, nearT = sb("d_near", [P, NP, P]), sb("d_nearT", [P, NP, P])
        nmax = sb("d_nmax", [P, NR])
        out = sb("d_out", [P, 2, P])
        ident, qmask, fmask = sb("d_ident", [P, P]), sb("d_qmask", [P, P]), sb("d_fmask", [P, 2, P])
        tabq, tabk, tabv = sb("d_tabq", [QR, P + 1], BF16), sb("d_tabk", [KR, 2, 3 * P], BF16), sb("d_tabv", [P, 2, VW])
        lg = [ctx.enter_context(nc.psum_tensor(f"d_lg{n}", [P, S], F32)) for n in range(2)]
        tp = [ctx.enter_context(nc.psum_tensor(f"d_tp{n}", [P, 512], F32)) for n in range(2)]
        po = ctx.enter_context(nc.psum_tensor("d_po", [P, 512], F32))
        pk = ctx.enter_context(nc.psum_tensor("d_pk", [P, 512], F32))
        ql = pk[:, 0:QL_PER_STEP * (P + 1)].rearrange("p (k x) -> p k x", k=QL_PER_STEP)

        consts, cleared, band_cleared = sem("d_consts"), sem("d_cleared"), sem("d_band_cleared")
        carrier = sem("d_carrier")
        q_in, k_in = [sem(f"d_q_in{n}") for n in range(GH)], sem("d_k_in")
        head_in = [sem(f"d_head_in{n}") for n in range(2)]
        val_in = [sem(f"d_val_in{n}") for n in range(2)]
        ql_done, ql_ready = sem("d_ql_done"), sem("d_ql_ready")
        skew_out = [sem(f"d_skew_out{n}") for n in range(GH)]
        skew_in = sem("d_skew_in")
        rq_done, band_ready = sem("d_rq_done"), sem("d_band_ready")
        lg_done, lg_added, max_ready, prob_ready = (sem(f"d_{n}") for n in ("lgd", "lga", "maxr", "probr"))
        tp_done, tp_read, near_done, near_read = (sem(f"d_{n}") for n in ("tpd", "tpr", "neard", "nearr"))
        win_out = [sem(f"d_win_out{n}") for n in range(NR // 2)]
        near_in = [sem(f"d_near_in{n}") for n in range(NP // 2)]
        far_ready, pv_done, out_ready = (sem(f"d_{n}") for n in ("farr", "pvd", "outr"))
        out_stored = [sem(f"d_out_stored{n}") for n in range(2)]
        const_loads = [(ident[:], i["ident"]), (qmask[:], i["qmask"]), (fmask[:], i["fmask"]), (tabq[:], scr.tabq),
                       (tabk[:], scr.tabk.rearrange("c k n -> k c n")), (tabv[:], scr.tabv.rearrange("c p n -> p c n"))]

        def window(t):
            a, z = max(0, t * P - PAD), min(S, t * P + P + PAD)
            return a, z, a - (t * P - PAD)

        def windows(k):
            both = prob[:, k % NR:k % NR + 2, (k % NT) * P:(k % NT) * P + WIN]
            return bass.AP(both.tensor, both.offset, [both.ap[0], [S + 2 * PAD + P, 2], [1, WIN]])

        def ql_tiles(n):
            k = QL_PER_STEP * (n - QL_FROM)
            return range(max(0, k), max(0, min(ST, k + QL_PER_STEP)))

        def opnd_rows(op, g, j):
            return bass.AP(scr.opnd.tensor, op * SLOTS * B * D * S + (GH * g + j) * (HD * S),
                           [[B * D * S, SLOTS], [S, HD], [1, S]])

        def over_groups(eng, main, prefetch):
            for n in range(ST):
                prefetch(0, n, 0)

            def steps(g, par):
                for n in range(ST):
                    main(g, n, par)
                    prefetch(g + 1, n, 1 - par)

            steps(0, 0)
            with eng.Fori(0, (NG - 2) // 2) as pair:
                steps(2 * pair + 1, 1)
                steps(2 * pair + 2, 0)
            for n in range(END):
                main(NG - 1, n, 1)

        def lag(g, n, by):
            k = n - by
            return None if k >= ST or (isinstance(g, int) and g == 0 and k < 0) else k

        with nc.Block() as block:
            @block.sync
            def _(sp):
                def load_group(g, par, n):
                    j = n % GH
                    if n < GH:
                        sp.dma_start(q128[0:KR, par, j, :], opnd_rows(Q128, g, j)).then_inc(q_in[j], 16)
                    else:
                        sp.dma_start(k128[:, par, j, PAD:PAD + S], opnd_rows(K128, g, j)).then_inc(k_in, 16)

                def load_head(g, j, n):
                    dst, op = (q0, Q0) if n == 0 else (k0, K0)
                    sp.dma_start(dst[:, j % 2, :], opnd_rows(op, g, j)).then_inc(head_in[j % 2], 16)

                def load_vals(g, j):
                    sp.dma_start(vals[:, j % 2].rearrange("p t c n -> p (t c n)"),
                                 scr.vals.rearrange("g p t c n -> g p (t c n)")[GH * g + j]).then_inc(val_in[j % 2], 16)

                def prefetch(g, n, par):
                    for j in range(GH):
                        at = QL_FROM - (-NT * (j + 1) // QL_PER_STEP)
                        if n == at:
                            sp.wait_ge(ql_ready, QL_STEPS * g + at - QL_FROM)
                            sp.dma_start(scr.skew[j][:, :, 0:P], qlin[:, j]).then_inc(skew_out[j], 16)
                        if n == at + 2:
                            ge(sp, lg_added, ST * (g - 1))
                            sp.wait_ge(skew_out[j], 16 * (g + 1))
                            for k in range(4):
                                src = bass.AP(scr.skew.tensor, (j * P + 32 * k) * NT * 2 * P,
                                              [[NT * 2 * P - 1, 32], [2 * P, NT], [1, P + 32]])
                                sp.dma_start(band[32 * k:32 * k + 32, par, j, :, 32 * k:32 * k + P + 32],
                                             src).then_inc(skew_in, 16)

                def main(g, n, par):
                    k = lag(g, n, LE + 1)
                    if k is not None and k % 2 == 0:
                        if not (isinstance(g, int) and g == 0 and k < NP):
                            sp.wait_ge(near_in[k // 2 % (NP // 2)], 16 * (ST // NP * g + k // NP))
                            sp.sem_inc(carrier, 1)
                        sp.wait_ge(prob_ready, ST * g + k + 2)
                        sp.dma_start(scr.prow[k % NP:k % NP + 2].rearrange("a p w -> p a w"), windows(k)
                                     ).then_inc(win_out[k // 2 % (NR // 2)], 16)
                    k = lag(g, n, LE + 2)
                    if k is not None and k % 2 == 0:
                        ge(sp, near_done, ST * g + k - NP + 2)
                        sp.sem_inc(carrier, 1)
                        sp.wait_ge(win_out[k // 2 % (NR // 2)], 16 * (ST // NR * g + k // NR + 1))
                        src = bass.AP(scr.prow.tensor, (k % NP) * P * WIN, [[WIN + 1, P], [P * WIN, 2], [1, P]])
                        sp.dma_start(near[:, k % NP:k % NP + 2, :], src).then_inc(near_in[k // 2 % (NP // 2)], 16)
                    k = lag(g, n, LP + 1)
                    if k is not None and k % QD == QD - 1:
                        q = k // QD
                        sp.wait_ge(out_ready, NQ * g + q + 1)
                        sp.sem_inc(carrier, 1)
                        sp.dma_start(scr.attn.rearrange("h q p l -> (h q) p l")[NQ * g + q], out[:, q % 2]
                                     ).then_inc(out_stored[q % 2], 16)
                    if n < 2 * GH and not (isinstance(g, int) and g == NG - 1):
                        if n == 0:
                            ge(sp, lg_done, ST * g)
                            sp.wait_ge(rq_done, NCH * (g + 1))
                            sp.sem_inc(carrier, 1)
                        load_group(g + 1, 1 - par, n)
                    j = n // NT
                    more = n < ST and not (isinstance(g, int) and g == NG - 1 and j == GH - 1)
                    if more and n % NT < 2:
                        ge(sp, lg_done, ST * g + NT * j)
                        load_head(g + (j + 1) // GH, (j + 1) % GH, n % NT)
                    if more and n % NT == LP:
                        ge(sp, pv_done, NQ * g + NQH * j)
                        load_vals(g + (j + 1) // GH, (j + 1) % GH)

                for dst, src in const_loads:
                    sp.dma_start(dst, src).then_inc(consts, 16)
                for n in range(2):
                    load_head(0, 0, n)
                load_vals(0, 0)
                sp.wait_ge(cleared, 1)
                for n in range(2 * GH):
                    load_group(0, 0, n)
                sp.wait_ge(band_cleared, 2)
                over_groups(sp, main, prefetch)
                for k in range(2):
                    sp.wait_ge(out_stored[k], 16 * NG * NQ // 2)

            @block.tensor
            def _(pe):
                t = nc.tensor

                def prefetch(g, n, par):
                    tiles = ql_tiles(n)
                    k = n - RQ_FROM
                    if tiles or 0 <= k < NCH:
                        ge(pe, ql_ready, QL_STEPS * g + min(n - QL_FROM, QL_STEPS))
                        ge(pe, band_ready, NCH * g + max(0, k))
                    if k == 0:
                        pe.wait_ge(k_in, 16 * GH * (g + 1))
                    for q in tiles:
                        if q % NT == 0:
                            pe.wait_ge(q_in[q // NT], 16 * (g + 1))
                        last = t.matmul(ql[:, q % QL_PER_STEP, :], q128[:, par, q // NT, (q % NT) * P:(q % NT + 1) * P], tabq[:],
                                        start=True, stop=True)
                    if tiles:
                        last.then_inc(ql_done, 1)
                    if 0 <= k < NCH:
                        for a in range(RQ_W):
                            w = RQ_W * k + a
                            keys = k128[:, par].rearrange("k h (t c) -> k h t c", c=P)[:, :, w // P:w // P + NT, w % P]
                            last = t.matmul(pk[:, a * GH * NT:(a + 1) * GH * NT], tabk[:, w // P, WIN - w:WIN - w + P], keys,
                                            start=True, stop=True)
                        last.then_inc(rq_done, 1)

                def main(g, n, par):
                    if n < ST:
                        j, row = n // NT, n % NT
                        if row == 0:
                            pe.wait_ge(head_in[j % 2], 32 * (2 * g + j // 2 + 1))
                        ge(pe, prob_ready, ST * g + n - 1)
                        split = row * P + PAD
                        for a, z in ((0, min(split, 512)), (512, split), (split, 512), (max(split, 512), S)):
                            if z > a:
                                base0 = a >= split
                                q = q0[:, j % 2, :] if base0 else q128[0:KR, par, j, :]
                                keys = k0[:, j % 2, a:z] if base0 else k128[:, par, j, PAD + a:PAD + z]
                                last = t.matmul(lg[n % 2][:, a:z], q[:, row * P:(row + 1) * P], keys, start=True, stop=True)
                        last.then_inc(lg_done, 1)
                    k = lag(g, n, LT)
                    if k is not None:
                        pe.wait_ge(prob_ready, ST * g + k + 1)
                        for half in range(2):
                            ge(pe, tp_read, 2 * (ST * g + k) + half - 1)
                            if half == 0:
                                ge(pe, near_read, ST * g + k + LT - LU)
                            for a in range(4):
                                c0 = PAD + (4 * half + a) * P
                                last = t.transpose(tp[half][:, a * P:(a + 1) * P], prob[:, k % NR, c0:c0 + P], ident[:])
                            last.then_inc(tp_done, 1)
                    k = lag(g, n, LP)
                    if k is not None:
                        q, at = k // QD, k % QD
                        hd = q // NQH
                        if at == 0:
                            ge(pe, out_ready, NQ * g + q)
                            if q % NQH == 0:
                                pe.wait_ge(val_in[hd % 2], 16 * (2 * g + hd // 2 + 1))
                            pe.wait_ge(tp_read, 2 * (ST * g + QD * (q + 1)))
                        for what in QUAD_STEPS[at]:
                            if what == "far":
                                pe.wait_ge(far_ready, ST * g + QD * (q + 1))
                            if what == "near":
                                pe.wait_ge(near_read, ST * g + QD * (q + 1))
                            for c in range(QD):
                                tile = QD * q + c
                                if what == "far":
                                    table, probs = tabv[:, 1, :], far[:, tile % NP, :]
                                elif what == "near":
                                    table, probs = tabv[:, 0, :], nearT[:, tile % NP, :]
                                else:
                                    base = 0 if what <= tile % NT - 2 else 1
                                    table, probs = vals[:, hd % 2, what, base, :], probT[:, tile % NP, what, :]
                                last = t.matmul(po[CG * c:CG * c + VW, 0:P], table, probs,
                                                start=what == 0, stop=what == "near")
                        if at == QD - 1:
                            last.then_inc(pv_done, 1)
                    k = lag(g, n, LU)
                    if k is not None:
                        pe.wait_ge(near_in[k // 2 % (NP // 2)], 16 * (ST // NP * g + k // NP + 1))
                        pe.wait_ge(tp_read, 2 * (ST * g + min(n - LT, ST - 1)) + 1)
                        if n - LT >= ST:
                            pe.wait_ge(near_read, ST * g + k)
                        t.transpose(tp[0][:, 0:P], near[:, k % NP, :], ident[:]).then_inc(near_done, 1)

                pe.wait_ge(consts, 16 * len(const_loads))
                pe.wait_ge(cleared, 1)
                over_groups(pe, main, prefetch)

            @block.scalar
            def _(act):
                a = nc.scalar

                def main(g, n, par):
                    k = lag(g, n, LE)
                    if k is not None:
                        ge(act, tp_done, 2 * (ST * g + k - NR + 1))
                        ge(act, win_out[k // 2 % (NR // 2)], 16 * (ST // NR * g + k // NR))
                        act.wait_ge(max_ready, ST * g + k + 1)
                        a.activation(prob[:, k % NR, PAD:PAD + S], lg[k % 2][:], ACT.Exp,
                                     bias=nmax[:, k % NR:k % NR + 1]).then_inc(prob_ready, 1)
                    k = lag(g, n, LT)
                    if k is not None:
                        ge(act, pv_done, NQ * g + k // QD - 1)
                        for half in range(2):
                            act.wait_ge(tp_done, 2 * (ST * g + k) + half + 1)
                            a.copy(probT[:, k % NP, 4 * half:4 * half + 4, :].rearrange("p a c -> p (a c)"),
                                   tp[half][:]).then_inc(tp_read, 1)
                    k = lag(g, n, LU)
                    if k is not None:
                        act.wait_ge(near_done, ST * g + k + 1)
                        a.copy(nearT[:, k % NP, :], tp[0][:, 0:P]).then_inc(near_read, 1)
                    k = lag(g, n, LP)
                    if k is not None and k % QD == QD - 1:
                        q = k // QD
                        ge(act, out_stored[q % 2], 16 * (NQ // 2 * g + q // 2))
                        act.wait_ge(pv_done, NQ * g + q + 1)
                        a.copy(out[:, q % 2], po[:, 0:P]).then_inc(out_ready, 1)

                act.wait_ge(cleared, 1)
                over_groups(act, main, lambda g, n, par: None)

            @block.gpsimd
            def _(pool):
                p = nc.gpsimd

                def main(g, n, par):
                    k = lag(g, n, LT)
                    if k is not None:
                        row, slot = k % NT, k % NP
                        ge(pool, pv_done, NQ * g + k // QD - 1)
                        pool.wait_ge(tp_read, 2 * (ST * g + k + 1))
                        if row == 0:
                            p.tensor_tensor(far[:, slot, :], probT[:, slot, 0, :], fmask[:, 1, :], ALU.mult).then_inc(far_ready, 1)
                        else:
                            ge(pool, far_ready, ST * g + k)
                            p.tensor_tensor(farm[:], probT[:, slot, row - 1:row + 1, :], fmask[:], ALU.mult)
                            pool.drain()
                            p.tensor_tensor(far[:, slot, :], farm[:, 0, :], farm[:, 1, :], ALU.add).then_inc(far_ready, 1)

                p.memset(band[:, 1], 0.0).then_inc(band_cleared, 1)
                pool.wait_ge(consts, 16 * len(const_loads))
                over_groups(pool, main, lambda g, n, par: None)

            @block.vector
            def _(dve):
                v = nc.vector

                def prefetch(g, n, par):
                    tiles = ql_tiles(n)
                    if tiles:
                        dve.wait_ge(ql_done, QL_STEPS * g + n - QL_FROM + 1)
                    for q in tiles:
                        j, row = q // NT, q % NT
                        if row == 0:
                            ge(dve, skew_out[j], 16 * g)
                        ins = v.scalar_tensor_tensor(qlin[:, j, row, :], qmask[:], ql[:, q % QL_PER_STEP, P:P + 1],
                                                     ql[:, q % QL_PER_STEP, 0:P], ALU.mult, ALU.add)
                    if tiles:
                        ins.then_inc(ql_ready, 1)
                    k = n - RQ_FROM
                    if 0 <= k < NCH:
                        if k == 0:
                            dve.wait_ge(skew_in, 16 * 4 * GH * (g + 1))
                        dve.wait_ge(rq_done, NCH * g + k + 1)
                        dst = band[:, par].rearrange("p h t w -> p (h t) w")[:, :, RQ_W * k:RQ_W * (k + 1)]
                        v.tensor_tensor(dst, pk[:].rearrange("p (w n) -> p n w", w=RQ_W), dst, ALU.add).then_inc(band_ready, 1)

                def main(g, n, par):
                    if n < ST:
                        if n == 0:
                            dve.wait_ge(band_ready, NCH * (g + 1))
                        a, z, at = window(n % NT)
                        dve.wait_ge(lg_done, ST * g + n + 1)
                        v.tensor_tensor(lg[n % 2][:, a:z], lg[n % 2][:, a:z],
                                        band[:, par, n // NT, n % NT, at:at + z - a], ALU.add).then_inc(lg_added, 1)
                        dve.wait_ge(lg_added, ST * g + n + 1)
                        v.tensor_reduce(nmax[:, n % NR:n % NR + 1], lg[n % 2][:], AX.X, ALU.max, negate=True).then_inc(max_ready, 1)

                for edge in (slice(0, PAD), slice(PAD + S, 2 * PAD + S)):
                    v.memset(k128[:, :, :, edge], 0.0)
                    v.memset(prob[:, :, edge], 0.0)
                v.memset(q128[KR:QR], 1.0)
                v.memset(po[:], 0.0)
                dve.drain()
                dve.sem_inc(cleared, 1)
                v.memset(band[:, 0], 0.0).then_inc(band_cleared, 1)
                dve.wait_ge(consts, 16 * len(const_loads))
                over_groups(dve, main, prefetch)


def combine_phase(nc, sem, i, scr, y):
    with ExitStack() as ctx:
        sb = lambda n, s, d=F32: ctx.enter_context(nc.sbuf_tensor(n, s, d))
        eo, xt = (sb(f"c_{n}", [P, 2, NT * D]) for n in ("eo", "x"))
        at = sb("c_at", [P, 2, H, NQH, P])
        rz = sb("c_rz", [P, 2, QD, QD])
        pos, prob = sb("c_pos", [P, 2, NT * E]), sb("c_prob", [P, 2, NT * E])
        iota_c, ident = sb("c_iota_c", [P, CAP]), sb("c_ident", [P, P])
        comb, combT = sb("c_comb", [P, 2, E, CAP]), sb("c_combT", [P, 2, E, P])
        base, res = sb("c_base", [P, 2, NT, D]), sb("c_res", [P, 2, NT, D])
        tp = [ctx.enter_context(nc.psum_tensor(f"c_tp{n}", [P, 512], F32)) for n in range(4)]
        po = [ctx.enter_context(nc.psum_tensor(f"c_po{n}", [P, 512], F32)) for n in range(2)]
        pa = [ctx.enter_context(nc.psum_tensor(f"c_pa{n}", [P, 512], F32)) for n in range(2)]
        consts = sem("c_consts")
        NA = H // QD * NQH
        at_done, at_read = sem("c_atd"), sem("c_atr")
        b_in, a_in = ([sem(f"c_{n}{k}") for k in range(2)] for n in ("in", "ain"))
        base_ready, comb_ready, tp_done, tp_read, o_done, res_ready = (
            sem(f"c_{n}") for n in ("baser", "combr", "tpd", "tpr", "od", "resr"))
        stored = sem("c_stored")
        carrier = sem("c_carrier")

        with nc.Block() as block:
            @block.sync
            def _(sp):
                def load_experts(b, s):
                    for dst, src in ((eo, scr.eout.rearrange("b c e d -> b c (e d)")), (pos, scr.pos), (prob, scr.prob)):
                        sp.dma_start(dst[:, s], src[b]).then_inc(b_in[s], 16)

                def load_attention(b, s):
                    for k in range(4):
                        sp.dma_start(at[:, s, k * H // 4:(k + 1) * H // 4].rearrange("p h q l -> p (h q) l"),
                                     scr.attn.rearrange("(b k h) q p l -> b k p (h q) l", b=B, k=4)[b, k]).then_inc(a_in[s], 16)
                    for k in range(2):
                        sp.dma_start(xt[:, s, k * NT * D // 2:(k + 1) * NT * D // 2].rearrange("p (t d) -> p t d", d=D),
                                     i["x"].rearrange("b (k t p) d -> b k p t d", k=2, p=P)[b, k]).then_inc(a_in[s], 16)

                def body(pair, last):
                    for s in range(2):
                        b = 2 * pair + s
                        if not last:
                            sp.wait_ge(base_ready, b + 1)
                            sp.sem_inc(carrier, 1)
                            load_attention(b + 2, s)
                        sp.wait_ge(res_ready, NT * (b + 1))
                        sp.sem_inc(carrier, 1)
                        sp.dma_start(y.rearrange("b (t p) d -> b p t d", p=P)[b], res[:, s]).then_inc(stored, 16)
                        if not last:
                            load_experts(b + 2, s)

                for dst, src in ((iota_c[:], i["iota_c"]), (ident[:], i["ident"])):
                    sp.dma_start(dst, src).then_inc(consts, 16)
                for s in range(2):
                    load_attention(s, s)
                    load_experts(s, s)
                batch_pairs(sp, body)
                sp.wait_ge(stored, 16 * B)

            @block.tensor
            def _(pe):
                t = nc.tensor

                def attention(b, s, u):
                    ge(pe, at_read, NA * b + u - 1)
                    for h in range(QD):
                        last = t.transpose(pa[u % 2][:, h * P:(h + 1) * P], at[:, s, QD * (u // NQH) + h, u % NQH, :], ident[:])
                    last.then_inc(at_done, 1)

                def turn(b, n):
                    ge(pe, comb_ready, NT * b + n + 1)
                    for half in range(2):
                        bank = tp[2 * (n % 2) + half]
                        ge(pe, tp_read, 2 * (NT * b + n - 2) + half + 1)
                        for a in range(4):
                            last = t.transpose(bank[:, a * P:(a + 1) * P], comb[:, n % 2, 4 * half + a, :], ident[:])
                        last.then_inc(tp_done, 1)

                def body(pair, last_pair):
                    for s in range(2):
                        b, more = 2 * pair + s, not (last_pair and s == 1)
                        for n in range(NT):
                            if n + 1 < NT:
                                turn(b, n + 1)
                            elif more:
                                turn(b + 1, 0)
                            ge(pe, tp_read, 2 * (NT * b + n + 1))
                            ge(pe, res_ready, NT * b + n - 1)
                            if n == 0:
                                ge(pe, b_in[s], 48 * (pair + 1))
                            for e in range(E):
                                last = t.matmul(po[n % 2][:, 0:D], combT[:, n % 2, e, :], eo[:, s, e * D:(e + 1) * D],
                                                start=e == 0, stop=e == E - 1)
                            last.then_inc(o_done, 1)
                            if more:
                                if n == 0:
                                    ge(pe, a_in[1 - s], 96 * (pair + s + 1))
                                attention(b + 1, 1 - s, n)

                pe.wait_ge(consts, 32)
                pe.wait_ge(a_in[0], 96)
                for u in range(NA):
                    attention(0, 0, u)
                turn(0, 0)
                batch_pairs(pe, body)

            @block.scalar
            def _(act):
                def body(b):
                    for n in range(NT):
                        for half in range(2):
                            ge(act, tp_done, 2 * (NT * b + n) + half + 1)
                            if half == 0:
                                ge(act, o_done, NT * b + n - 1)
                            nc.scalar.copy(combT[:, n % 2, 4 * half:4 * half + 4, :].rearrange("p a c -> p (a c)"),
                                           tp[2 * (n % 2) + half][:]).then_inc(tp_read, 1)

                turns(act, B, body)

            @block.gpsimd
            def _(pool):
                def body(pair, last):
                    for s in range(2):
                        b = 2 * pair + s
                        ge(pool, a_in[s], 96 * (pair + 1))
                        ge(pool, at_read, NA * (b + 1))
                        sums = base[:, s].rearrange("p t d -> p (t d)")
                        nc.gpsimd.tensor_tensor(sums, sums, xt[:, s], ALU.add).then_inc(base_ready, 1)

                batch_pairs(pool, body)

            @block.vector
            def _(dve):
                v = nc.vector

                def attention(b, s, u):
                    ge(dve, at_done, NA * b + u + 1)
                    sums = pa[u % 2][:].rearrange("p (h t c) -> p h t c", h=QD, t=QD)
                    v.reciprocal(rz[:, u % 2], sums[:, :, :, HD])
                    dve.drain()
                    hc, qd = u // NQH, u % NQH
                    dst = base[:, s, QD * qd:QD * (qd + 1), QD * HD * hc:QD * HD * (hc + 1)]
                    v.tensor_tensor(dst.rearrange("p t (h d) -> p h t d", h=QD), sums[:, :, :, 0:HD],
                                    rz[:, u % 2].rearrange("p h (t a) -> p h t a", a=1).to_broadcast([P, QD, QD, HD]),
                                    ALU.mult).then_inc(at_read, 1)

                def spread(b, s, n):
                    ge(dve, tp_done, 2 * (NT * b + n - 1))
                    for e in range(E):
                        k = n * E + e
                        ins = v.tensor_scalar(comb[:, n % 2, e, :], iota_c[:], pos[:, s, k:k + 1],
                                              prob[:, s, k:k + 1], ALU.is_equal, ALU.mult)
                    ins.then_inc(comb_ready, 1)

                def body(pair, last):
                    for s in range(2):
                        b, more = 2 * pair + s, not (last and s == 1)
                        for n in range(NT):
                            if n + 2 < NT:
                                spread(b, s, n + 2)
                            elif more:
                                if n + 2 == NT:
                                    ge(dve, b_in[1 - s], 48 * (pair + s + 1))
                                spread(b + 1, 1 - s, n + 2 - NT)
                            if n == 0:
                                ge(dve, base_ready, b + 1)
                                ge(dve, stored, 16 * (b - 1))
                            ge(dve, o_done, NT * b + n + 1)
                            v.tensor_tensor(res[:, s, n, :], po[n % 2][:, 0:D], base[:, s, n, :], ALU.add).then_inc(res_ready, 1)
                            if more:
                                attention(b + 1, 1 - s, n)

                dve.wait_ge(consts, 32)
                dve.wait_ge(b_in[0], 48)
                spread(0, 0, 0)
                spread(0, 0, 1)
                for u in range(NA):
                    attention(0, 0, u)
                batch_pairs(dve, body)


def build(nc, ins, y, upto=5):
    with ExitStack() as ctx:
        sem = lambda name: ctx.enter_context(nc.semaphore(name))
        scr = Scratch(nc)
        tokens_phase(nc, sem, ins, scr)
        if upto > 2:
            experts_phase(nc, sem, ins, scr)
        if upto > 3:
            attend_phase(nc, sem, ins, scr)
        if upto > 4:
            combine_phase(nc, sem, ins, scr, y)


def layouts(x, Wq, Wk, Wv, Eq, Ek, Ev, wr, wi, wo):
    f = lambda a: np.ascontiguousarray(np.asarray(a))
    Eq, Ek, Ev = f(Eq), f(Ek), f(Ev)
    N = 2 * MAXD
    rev = N - np.arange(P + 1)
    clipped = np.clip(np.arange(3 * P) - P, 0, N)
    head_rows = lambda a: np.tile(a, H)
    marks = np.zeros((KR, 6), np.float32)
    for r in range(KR):
        marks[r, Q_SLOTS[r // HD]] = 1
        marks[r, 3 + K_SLOTS[r // HD]] = 1
    p, c = np.arange(P)[:, None], np.arange(P)[None, :]
    fmask = np.stack([c + MAXD > p, c - MAXD > p], 1).astype(np.float32)
    return {
        "x": f(x), "wq": f(Wq), "wk": f(Wk), "wv": f(Wv), "wr": f(wr), "wi": f(wi), "wo": f(wo),
        "ekx": f(np.tile(Ek[rev].T, (SLOTS, 1))), "eqx": f(np.tile(Eq[rev].T, (SLOTS, 1))),
        "equ": f(np.tile(Eq[clipped].T, (SLOTS, 1))),
        "eqk_cols": f(np.stack([np.tile(a, P // HD) for a in (Eq[N], Eq[0], Ek[N], Ek[0])], 1)),
        "evx": f(Ev[rev[:P]]),
        "ev_rows": f(np.broadcast_to(np.stack([head_rows(Ev[N]), head_rows(Ev[0])])[None], (P, 2, D))),
        "marks": marks,
        "ident": np.eye(P, dtype=np.float32),
        "iota_c": f(np.broadcast_to(np.arange(CAP, dtype=np.float32), (P, CAP))),
        "iota_e": f(np.broadcast_to(np.tile(np.arange(E, dtype=np.float32), NT), (P, NT * E))),
        "upper": f(np.concatenate([(p <= c), np.ones((P, P))], 1).astype(np.float32)),
        "qmask": (p + c >= P).astype(np.float32),
        "fmask": f(fmask),
    }


def program(arrays, nc, upto=5):
    ins = {n: nc.dram_tensor(f"in_{n}", a.shape, mybir.dt.from_np(a.dtype), kind="ExternalInput").ap()
           for n, a in arrays.items()}
    y = nc.dram_tensor("out_y", (B, S, D), F32, kind="ExternalOutput").ap()
    build(nc, ins, y, upto)


def kernel(**inputs):
    import concourse.bacc as bacc
    from concourse.bass_utils import run_bass_kernel_spmd

    names = ["L0_attn_x", "L0_attn_Wq", "L0_attn_Wk", "L0_attn_Wv", "L0_attn_Eq", "L0_attn_Ek", "L0_attn_Ev",
             "L0_ffn_w_router", "L0_ffn_wi", "L0_ffn_wo"]
    arrays = layouts(*[inputs[n] for n in names])
    nc = bacc.Bacc("TRN2", target_bir_lowering=False, num_devices=1)
    program(arrays, nc)
    got = run_bass_kernel_spmd(nc, [{f"in_{n}": a for n, a in arrays.items()}], core_ids=[0])
    return got.results[0]["out_y"]
```
